# Optimizing a Trainium2 kernel written in Bass

```python
import numpy as np
import jax
import jax.numpy as jnp

def _softmax(x, axis=-1):
    return jax.nn.softmax(x, axis=axis)

def _gelu(x):
    return jax.nn.gelu(x, approximate=True)

def _silu(x):
    return jax.nn.silu(x)

def _sigmoid(x):
    return jax.nn.sigmoid(x)

def _layernorm(x, axis=-1, eps=1e-05):
    m = jnp.mean(x, axis=axis, keepdims=True)
    v = jnp.var(x, axis=axis, keepdims=True)
    return (x - m) / jnp.sqrt(v + eps)

def _scatter_add(tgt, idx, src, axis=0):
    return tgt.at[idx].add(src)

def _segment_sum(src, seg, n):
    return jax.ops.segment_sum(src, seg, n)
kernel_name = 'mk_dlrm_tower_d1_rec_r8_7a28a4'

def setup_inputs(seed: int=0):
    np.random.seed(seed)
    _w = jnp.asarray

    def _rec_inputs():
        import jax
        import jax.numpy as jnp
        _tk = jax.random.key(seed)
        dense_ctx = jax.random.normal(jax.random.fold_in(_tk, 190), (512, 16), jnp.float32)
        ids = jnp.stack([jax.random.randint(jax.random.fold_in(_tk, 200 + f), (512,), 0, v, jnp.int32) for f, v in enumerate([1250, 125000, 125000, 1250, 1000, 1000, 12500, 12500, 1250, 1250, 1250, 1250, 125000, 1000, 125000, 1000, 12500, 12500, 1250, 1250, 125000, 125000, 1250, 125000, 1000, 1000])], axis=1)
        tbl_0 = 0.05 * jax.random.normal(jax.random.fold_in(_tk, 500 + 0), (1250, 32), jnp.float32)
        tbl_1 = 0.05 * jax.random.normal(jax.random.fold_in(_tk, 500 + 1), (125000, 32), jnp.float32)
        tbl_2 = 0.05 * jax.random.normal(jax.random.fold_in(_tk, 500 + 2), (125000, 32), jnp.float32)
        tbl_3 = 0.05 * jax.random.normal(jax.random.fold_in(_tk, 500 + 3), (1250, 32), jnp.float32)
        tbl_4 = 0.05 * jax.random.normal(jax.random.fold_in(_tk, 500 + 4), (1000, 32), jnp.float32)
        tbl_5 = 0.05 * jax.random.normal(jax.random.fold_in(_tk, 500 + 5), (1000, 32), jnp.float32)
        tbl_6 = 0.05 * jax.random.normal(jax.random.fold_in(_tk, 500 + 6), (12500, 32), jnp.float32)
        tbl_7 = 0.05 * jax.random.normal(jax.random.fold_in(_tk, 500 + 7), (12500, 32), jnp.float32)
        tbl_8 = 0.05 * jax.random.normal(jax.random.fold_in(_tk, 500 + 8), (1250, 32), jnp.float32)
        tbl_9 = 0.05 * jax.random.normal(jax.random.fold_in(_tk, 500 + 9), (1250, 32), jnp.float32)
        tbl_10 = 0.05 * jax.random.normal(jax.random.fold_in(_tk, 500 + 10), (1250, 32), jnp.float32)
        tbl_11 = 0.05 * jax.random.normal(jax.random.fold_in(_tk, 500 + 11), (1250, 32), jnp.float32)
        tbl_12 = 0.05 * jax.random.normal(jax.random.fold_in(_tk, 500 + 12), (125000, 32), jnp.float32)
        tbl_13 = 0.05 * jax.random.normal(jax.random.fold_in(_tk, 500 + 13), (1000, 32), jnp.float32)
        tbl_14 = 0.05 * jax.random.normal(jax.random.fold_in(_tk, 500 + 14), (125000, 32), jnp.float32)
        tbl_15 = 0.05 * jax.random.normal(jax.random.fold_in(_tk, 500 + 15), (1000, 32), jnp.float32)
        tbl_16 = 0.05 * jax.random.normal(jax.random.fold_in(_tk, 500 + 16), (12500, 32), jnp.float32)
        tbl_17 = 0.05 * jax.random.normal(jax.random.fold_in(_tk, 500 + 17), (12500, 32), jnp.float32)
        tbl_18 = 0.05 * jax.random.normal(jax.random.fold_in(_tk, 500 + 18), (1250, 32), jnp.float32)
        tbl_19 = 0.05 * jax.random.normal(jax.random.fold_in(_tk, 500 + 19), (1250, 32), jnp.float32)
        tbl_20 = 0.05 * jax.random.normal(jax.random.fold_in(_tk, 500 + 20), (125000, 32), jnp.float32)
        tbl_21 = 0.05 * jax.random.normal(jax.random.fold_in(_tk, 500 + 21), (125000, 32), jnp.float32)
        tbl_22 = 0.05 * jax.random.normal(jax.random.fold_in(_tk, 500 + 22), (1250, 32), jnp.float32)
        tbl_23 = 0.05 * jax.random.normal(jax.random.fold_in(_tk, 500 + 23), (125000, 32), jnp.float32)
        tbl_24 = 0.05 * jax.random.normal(jax.random.fold_in(_tk, 500 + 24), (1000, 32), jnp.float32)
        tbl_25 = 0.05 * jax.random.normal(jax.random.fold_in(_tk, 500 + 25), (1000, 32), jnp.float32)
        _rk = jax.random.fold_in(_tk, 7)
        W_top1 = 0.0606339 * jax.random.normal(jax.random.fold_in(_tk, 801), (272, 512), jnp.float32)
        W_top2 = 0.0441942 * jax.random.normal(jax.random.fold_in(_tk, 802), (512, 256), jnp.float32)
        W_top3 = 0.0625 * jax.random.normal(jax.random.fold_in(_tk, 803), (256, 1), jnp.float32)
        b_top1 = jnp.zeros((512,), jnp.float32)
        b_top2 = jnp.zeros((256,), jnp.float32)
        return (dense_ctx, ids, tbl_0, tbl_1, tbl_2, tbl_3, tbl_4, tbl_5, tbl_6, tbl_7, tbl_8, tbl_9, tbl_10, tbl_11, tbl_12, tbl_13, tbl_14, tbl_15, tbl_16, tbl_17, tbl_18, tbl_19, tbl_20, tbl_21, tbl_22, tbl_23, tbl_24, tbl_25, W_top1, b_top1, W_top2, b_top2, W_top3)
    dense_ctx, ids, tbl_0, tbl_1, tbl_2, tbl_3, tbl_4, tbl_5, tbl_6, tbl_7, tbl_8, tbl_9, tbl_10, tbl_11, tbl_12, tbl_13, tbl_14, tbl_15, tbl_16, tbl_17, tbl_18, tbl_19, tbl_20, tbl_21, tbl_22, tbl_23, tbl_24, tbl_25, W_top1, b_top1, W_top2, b_top2, W_top3 = _rec_inputs()

    def _L0_rec_setup():
        import jax, jax.numpy as jnp
        import numpy as np
        M_FIELDS = 26
        H1 = 128
        H2 = 128
        BATCH = 256
        EMB_K = 32

        def _cin_layer(x_prev, x0, W, b):
            return jnp.einsum('bik,bjk,hij->bhk', x_prev, x0, W) + b[None, :, None]
        key = jax.random.key(seed)
        k0, k1, k2, k3, k4 = jax.random.split(key, 5)
        inputs = jax.random.normal(k0, (BATCH, M_FIELDS, EMB_K), dtype=jnp.float32)
        W1 = jax.random.normal(k1, (H1, M_FIELDS, M_FIELDS), dtype=jnp.float32) * 0.05
        b1 = jax.random.normal(k2, (H1,), dtype=jnp.float32) * 0.05
        W2 = jax.random.normal(k3, (H2, H1, M_FIELDS), dtype=jnp.float32) * 0.05
        b2 = jax.random.normal(k4, (H2,), dtype=jnp.float32) * 0.05
        return {'inputs': inputs, 'W1': W1, 'b1': b1, 'W2': W2, 'b2': b2}
    _L0_rec_all = _L0_rec_setup()
    _L0_rec_in = {k: v for k, v in _L0_rec_all.items() if k in ('W1', 'b1', 'W2', 'b2')}
    del _L0_rec_all
    return {'dense_ctx': dense_ctx, 'ids': ids, 'tbl_0': tbl_0, 'tbl_1': tbl_1, 'tbl_2': tbl_2, 'tbl_3': tbl_3, 'tbl_4': tbl_4, 'tbl_5': tbl_5, 'tbl_6': tbl_6, 'tbl_7': tbl_7, 'tbl_8': tbl_8, 'tbl_9': tbl_9, 'tbl_10': tbl_10, 'tbl_11': tbl_11, 'tbl_12': tbl_12, 'tbl_13': tbl_13, 'tbl_14': tbl_14, 'tbl_15': tbl_15, 'tbl_16': tbl_16, 'tbl_17': tbl_17, 'tbl_18': tbl_18, 'tbl_19': tbl_19, 'tbl_20': tbl_20, 'tbl_21': tbl_21, 'tbl_22': tbl_22, 'tbl_23': tbl_23, 'tbl_24': tbl_24, 'tbl_25': tbl_25, 'W_top1': W_top1, 'b_top1': b_top1, 'W_top2': W_top2, 'b_top2': b_top2, 'W_top3': W_top3, 'L0_rec_W1': _L0_rec_in['W1'], 'L0_rec_b1': _L0_rec_in['b1'], 'L0_rec_W2': _L0_rec_in['W2'], 'L0_rec_b2': _L0_rec_in['b2']}

def reference(dense_ctx, ids, tbl_0, tbl_1, tbl_2, tbl_3, tbl_4, tbl_5, tbl_6, tbl_7, tbl_8, tbl_9, tbl_10, tbl_11, tbl_12, tbl_13, tbl_14, tbl_15, tbl_16, tbl_17, tbl_18, tbl_19, tbl_20, tbl_21, tbl_22, tbl_23, tbl_24, tbl_25, W_top1, b_top1, W_top2, b_top2, W_top3, L0_rec_W1, L0_rec_b1, L0_rec_W2, L0_rec_b2):
    import jax
    import jax.numpy as jnp

    def _L0_rec_ref(inputs, W1, b1, W2, b2):
        import jax, jax.numpy as jnp
        import numpy as np
        M_FIELDS = 26
        H1 = 128
        H2 = 128
        BATCH = 256
        EMB_K = 32

        def _cin_layer(x_prev, x0, W, b):
            return jnp.einsum('bik,bjk,hij->bhk', x_prev, x0, W) + b[None, :, None]
        x1 = _cin_layer(inputs, inputs, W1, b1)
        x2 = _cin_layer(x1, inputs, W2, b2)
        res = jnp.concatenate([x1, x2], axis=1)
        return jnp.sum(res, axis=-1)
    e = jnp.stack([tbl_0[ids[:, 0]], tbl_1[ids[:, 1]], tbl_2[ids[:, 2]], tbl_3[ids[:, 3]], tbl_4[ids[:, 4]], tbl_5[ids[:, 5]], tbl_6[ids[:, 6]], tbl_7[ids[:, 7]], tbl_8[ids[:, 8]], tbl_9[ids[:, 9]], tbl_10[ids[:, 10]], tbl_11[ids[:, 11]], tbl_12[ids[:, 12]], tbl_13[ids[:, 13]], tbl_14[ids[:, 14]], tbl_15[ids[:, 15]], tbl_16[ids[:, 16]], tbl_17[ids[:, 17]], tbl_18[ids[:, 18]], tbl_19[ids[:, 19]], tbl_20[ids[:, 20]], tbl_21[ids[:, 21]], tbl_22[ids[:, 22]], tbl_23[ids[:, 23]], tbl_24[ids[:, 24]], tbl_25[ids[:, 25]]], axis=1)
    z = _L0_rec_ref(e, L0_rec_W1, L0_rec_b1, L0_rec_W2, L0_rec_b2)
    z = z.reshape(z.shape[0], -1)
    h = jnp.concatenate([z, dense_ctx], axis=1)
    h = jnp.maximum(h @ W_top1 + b_top1, 0.0)
    h = jnp.maximum(h @ W_top2 + b_top2, 0.0)
    y = h @ W_top3
    return y

_drawn_inputs = setup_inputs


def setup_inputs(seed=0):
    import zlib

    import numpy as np

    out = dict(_drawn_inputs(seed))
    spreads = {'b_top1': (0.0, 2.0), 'b_top2': (0.0, 0.8)}
    factors = {'tbl_0': 8.0,
     'tbl_1': 8.0,
     'tbl_2': 8.0,
     'tbl_3': 8.0,
     'tbl_4': 8.0,
     'tbl_5': 8.0,
     'tbl_6': 8.0,
     'tbl_7': 8.0,
     'tbl_8': 8.0,
     'tbl_9': 8.0,
     'tbl_10': 8.0,
     'tbl_11': 8.0,
     'tbl_12': 8.0,
     'tbl_13': 8.0,
     'tbl_14': 8.0,
     'tbl_15': 8.0,
     'tbl_16': 8.0,
     'tbl_17': 8.0,
     'tbl_18': 8.0,
     'tbl_19': 8.0,
     'tbl_20': 8.0,
     'tbl_21': 7.684,
     'tbl_22': 8.0,
     'tbl_23': 8.0,
     'tbl_24': 8.0,
     'tbl_25': 8.0,
     'L0_rec_W1': 8.0,
     'L0_rec_W2': 4.243,
     'dense_ctx': 6.358}
    for name, (base, spread) in spreads.items():
        noise = np.random.default_rng([zlib.crc32(name.encode()), seed]).standard_normal(out[name].shape)
        drawn = base * np.exp(spread * noise) if base else spread * noise
        out[name] = jnp.asarray(drawn.astype(out[name].dtype))
    for name, factor in factors.items():
        out[name] = (out[name] * factor).astype(out[name].dtype)
    return out
```

```python
from contextlib import ExitStack

import concourse.bass as bass
from concourse import mybir

F32 = mybir.dt.float32
U32 = mybir.dt.uint32
ALU = mybir.AluOpType
ACT = mybir.ActivationFunctionType


def dlrm_cin_tower(nc, dense_ctx, ids, tables, w_top1, b_top1, w_top2, b_top2, w_top3, w1, b1, w2, b2, out):
    P = 128
    BATCH, FIELDS = ids.shape
    K = tables[0].shape[1]
    H1, H2 = w1.shape[0], w2.shape[0]
    DENSE = dense_ctx.shape[1]
    TOP1, TOP2 = w_top2.shape
    TILES = BATCH // P
    QUADS = P // K
    BL = P // QUADS
    C = FIELDS // 2
    ND = C // 2 + 1
    WRAP = ND - 1
    LIN = C + WRAP
    PAIRS = ND * C
    ROWS = LIN + PAIRS
    COLS = FIELDS + 1
    GROUP = 4
    GROUPS = BL // GROUP
    EXT = 2 * C - 1
    CW = 2 * ROWS + 1
    MID1 = TOP1 // P
    MID2 = TOP2 // P
    CROSS = C * C
    PER_BANK = 512 // P
    assert (P, K, H1, H2) == (128, 32, 128, 128) and FIELDS == 2 * C and C % 2 == 1 and ROWS <= P

    with ExitStack() as ctx:
        def sb(name, shape, dt=F32):
            return ctx.enter_context(nc.sbuf_tensor(name, shape, dt))

        def bank(name):
            return ctx.enter_context(nc.psum_tensor(name, [P, 512], F32))

        def sem(name):
            return ctx.enter_context(nc.semaphore(name))

        ids_sb = sb("ids_sb", [P, TILES, FIELDS], U32)
        rows_sb = sb("rows_sb", [P, TILES, FIELDS * K])
        feat = sb("feat", [P, 2, 2, ROWS, BL])
        diag = sb("diag", [P, 2, BL, QUADS, COLS])
        mom = sb("mom", [ROWS, COLS, 2, P])
        coef = sb("coef", [P, FIELDS, CW])
        coefT = sb("coefT", [ROWS, FIELDS, 2, P])
        startup = feat[:, 1].rearrange("p c r b -> p (c r b)")
        w2_nat = startup[:, 0:H1 * FIELDS].rearrange("h (m l) -> h m l", l=FIELDS)
        w2T = startup[:, H1 * FIELDS:2 * H1 * FIELDS].rearrange("m (l h) -> m l h", l=FIELDS)
        w1_sb = sb("w1_sb", [P, FIELDS, FIELDS])
        w1s = sb("w1s", [P, CW])
        cross = sb("cross", [P, 2, EXT, C])
        bsum = sb("bsum", [P, 2, ROWS])
        bsumT = sb("bsumT", [ROWS, 2, P])
        w1T = sb("w1T", [ROWS, 2, P])
        crossT = sb("crossT", [C, C, P])
        ident = sb("ident", [P, P])
        bias_in = sb("bias_in", [P, 2])
        bias_z = sb("bias_z", [P, 2])
        dense_sb = sb("dense_sb", [P, TILES, DENSE])
        denseT = sb("denseT", [32, BATCH])
        wt1 = sb("wt1", [P, 2, TOP1])
        wt1d = sb("wt1d", [DENSE + 1, TOP1])
        wt2 = sb("wt2", [P, MID1, TOP2])
        wt3 = sb("wt3", [P, MID2])
        bt2 = sb("bt2", [P, MID2])
        z_sb = sb("z_sb", [P, 2, P])
        h1_sb = sb("h1_sb", [P, MID1 * P])
        h2_sb = sb("h2_sb", [P, MID2, P])
        y_sb = sb("y_sb", [1, BATCH])

        ring = [bank(f"ring{i}") for i in range(4)]
        z_ps = bank("z_ps")
        h1_ps = bank("h1_ps")
        h2_ps = bank("h2_ps")
        y_ps = bank("y_ps")

        s_ids = sem("s_ids")
        s_w1 = sem("s_w1")
        s_w2 = sem("s_w2")
        s_dense = sem("s_dense")
        s_top = sem("s_top")
        s_rows = [sem(f"s_rows{t}") for t in range(TILES)]
        s_zero = sem("s_zero")
        s_w1s = sem("s_w1s")
        s_w2T_pe = sem("s_w2T_pe")
        s_w2T = sem("s_w2T")
        s_own_pe = sem("s_own_pe")
        s_own = sem("s_own")
        s_other_pe = sem("s_other_pe")
        s_other = sem("s_other")
        s_bsum = sem("s_bsum")
        s_ct_pe = sem("s_ct_pe")
        s_ct_act = sem("s_ct_act")
        s_ct_dve = sem("s_ct_dve")
        s_dense_pe = sem("s_dense_pe")
        s_denseT = sem("s_denseT")
        s_fieldsT = sem("s_fieldsT")
        s_wrap = sem("s_wrap")
        s_pairs = sem("s_pairs")
        s_diag = sem("s_diag")
        s_mom_pe = sem("s_mom_pe")
        s_mom = sem("s_mom")
        s_z_pe = sem("s_z_pe")
        s_z = sem("s_z")
        s_h1_pe = sem("s_h1_pe")
        s_h1 = sem("s_h1")
        s_h2_pe = sem("s_h2_pe")
        s_h2 = sem("s_h2")
        s_y_pe = sem("s_y_pe")
        s_y = sem("s_y")
        s_out = sem("s_out")

        BANKS_W2T = -(-FIELDS // PER_BANK)
        OWN_PER_BANK = 2
        OTHER_PER_BANK = 3
        own_banks = [range(f, min(f + OWN_PER_BANK, FIELDS)) for f in range(0, FIELDS, OWN_PER_BANK)]
        other_banks = [range(f, min(f + OTHER_PER_BANK, FIELDS)) for f in range(0, FIELDS, OTHER_PER_BANK)]
        turns = [(coef[:, l, c * ROWS:(c + 1) * ROWS], ROWS, coefT[:, l, c, :])
                 for l in range(FIELDS) for c in range(2)]
        turn_banks = [(turns[n:n + PER_BANK], coefT[:, n // 2:n // 2 + PER_BANK // 2].rearrange(
            "r l c h -> r (l c h)")) for n in range(0, 2 * FIELDS, PER_BANK)]
        turn_banks.append(([(w1s[:, c * ROWS:(c + 1) * ROWS], ROWS, None) for c in range(2)],
                           w1T[:, :, :].rearrange("r c h -> r (c h)")))
        turn_banks.append(([(bsum[:, c, :], ROWS, None) for c in range(2)],
                           bsumT[:, :, :].rearrange("r c h -> r (c h)")))
        for l0 in range(0, C, PER_BANK):
            l1 = min(l0 + PER_BANK, C)
            turn_banks.append(([(cross[:, 0, WRAP:WRAP + C, l], C, None) for l in range(l0, l1)],
                               crossT[:, l0:l1, :].rearrange("i l h -> i (l h)")))

        def turned(eng, upto):
            eng.wait_ge(s_ct_act, (upto + 1) // 2)
            if upto // 2 > 0:
                eng.wait_ge(s_ct_dve, upto // 2)

        block = ctx.enter_context(nc.Block())

        @block.sync
        def _(sp):
            sp.dma_start(ids_sb[:, :, :], ids.bitcast(U32).rearrange("(t p) f -> p t f", p=P)).then_inc(s_ids, 16)
            sp.dma_start(w2_nat, w2).then_inc(s_w2, 16)
            sp.dma_start(w1_sb[:, :, :], w1).then_inc(s_w1, 16)
            with nc.allow_non_contiguous_dma(reason="a few hundred biases"):
                sp.dma_start(bias_in[:, 0:1], b1.rearrange("(p a) -> p a", a=1)).then_inc(s_w1, 16)
                sp.dma_start(bias_in[:, 1:2], b2.rearrange("(p a) -> p a", a=1)).then_inc(s_w1, 16)
                sp.dma_start(dense_sb[:, :, :], dense_ctx.rearrange("(t p) f -> p t f", p=P)).then_inc(s_dense, 16)
                sp.dma_start(wt1[:, :, :], w_top1[0:2 * P, :].rearrange("(c p) n -> p c n", p=P)).then_inc(s_top, 16)
                sp.dma_start(wt1d[0:DENSE, :], w_top1[2 * P:2 * P + DENSE, :]).then_inc(s_top, 16)
                sp.dma_start(wt1d[DENSE:DENSE + 1, :], b_top1.rearrange("(a n) -> a n", a=1)).then_inc(s_top, 16)
                sp.dma_start(wt2[:, :, :], w_top2.rearrange("(c p) n -> p c n", p=P)).then_inc(s_top, 16)
                sp.dma_start(wt3[:, :], w_top3.rearrange("(c p) a -> p (c a)", p=P)).then_inc(s_top, 16)
                sp.dma_start(bt2[:, :], b_top2.rearrange("(c p) -> p c", p=P)).then_inc(s_top, 16)
            sp.wait_ge(s_y, 1)
            sp.dma_start(out.rearrange("b a -> a b"), y_sb[:, :]).then_inc(s_out, 16)
            sp.wait_ge(s_out, 16)

        @block.gpsimd
        def _(pool):
            nc.gpsimd.memset(ident[:, :], 0.0).then_inc(s_zero, 1)
            pool.wait_ge(s_zero, 1)
            nc.gpsimd.affine_select(out=ident[:, :], in_=ident[:, :], compare_op=ALU.not_equal, fill=1.0, base=0,
                                    pattern=[[-1, P]], channel_multiplier=1).then_inc(s_zero, 1)
            pool.wait_ge(s_ids, 16)
            for t in range(TILES):
                for f in range(FIELDS):
                    nc.gpsimd.indirect_dma_start(
                        rows_sb[:, t, f * K:(f + 1) * K], None, tables[f],
                        bass.IndirectOffsetOnAxis(ap=ids_sb[:, t, f:f + 1], axis=0)).then_inc(s_rows[t], 16)

        @block.scalar
        def _(act):
            def copy_diag(t):
                act.wait_ge(s_fieldsT, t + 1)
                if t == 0:
                    act.wait_ge(s_w1s, 2)
                if t >= 2:
                    act.wait_ge(s_mom_pe, 2 * GROUPS * (t - 1))
                for q in range(QUADS):
                    src = feat[q * K:(q + 1) * K, t % 2, :, 0:C, :]
                    dst = diag[q * K:(q + 1) * K, t % 2, :, q, 0:FIELDS].rearrange("p b (c i) -> p c i b", c=2)
                    nc.scalar.copy(dst, src).then_inc(s_diag, 1)

            def copy_moments(t):
                for n in range(2 * GROUPS):
                    c, g = divmod(n, GROUPS)
                    act.wait_ge(s_mom_pe, 2 * GROUPS * t + n + 1)
                    if n == 0 and t >= 1:
                        act.wait_ge(s_z_pe, t)
                    src = ring[n % 4][0:ROWS, 0:GROUP * QUADS * COLS].rearrange(
                        "r (b q l) -> r b q l", b=GROUP, q=QUADS)
                    dst = mom[:, :, c, :].rearrange("r l (q g b) -> r g b q l", q=QUADS, b=GROUP)[:, g]
                    nc.scalar.copy(dst, src).then_inc(s_mom, 1)

            def copy_z(t):
                act.wait_ge(s_z_pe, t + 1)
                if t >= 1:
                    act.wait_ge(s_h1_pe, t)
                for n in range(2):
                    nc.scalar.activation(z_sb[:, n, :], z_ps[:, n * P:(n + 1) * P], ACT.Identity,
                                         bias=bias_z[:, n:n + 1]).then_inc(s_z, 1)

            for n in range(BANKS_W2T):
                f0, f1 = n * PER_BANK, min((n + 1) * PER_BANK, FIELDS)
                act.wait_ge(s_w2T_pe, n + 1)
                nc.scalar.copy(w2T[:, f0:f1, :].rearrange("m l h -> m (l h)"),
                               ring[n % 4][:, 0:(f1 - f0) * P]).then_inc(s_w2T, 1)
            for n, fs in enumerate(own_banks):
                act.wait_ge(s_own_pe, n + 1)
                nc.scalar.copy(coef[:, fs[0]:fs[-1] + 1, :].rearrange("h l r -> h (l r)"),
                               ring[n % 4][:, 0:len(fs) * CW]).then_inc(s_own, 1)
            copy_diag(0)
            copy_moments(0)
            for n, (group, dst) in enumerate(turn_banks):
                if n % 2 == 0:
                    act.wait_ge(s_ct_pe, n + 1)
                    nc.scalar.copy(dst, ring[n % 4][0:group[0][1], 0:len(group) * P]).then_inc(s_ct_act, 1)
            for t in range(1, TILES):
                copy_diag(t)
                if t == 1:
                    act.wait_ge(s_w1s, 3)
                copy_z(t - 1)
                copy_moments(t)
            copy_z(TILES - 1)

        @block.vector
        def _(dve):
            nc.vector.memset(w1s[:, :], 0.0).then_inc(s_w1s, 1)
            nc.vector.memset(diag[:, :, :, :, :].rearrange("p u b q l -> p (u b q l)"), 0.0)
            nc.vector.memset(bsum[:, :, :], 0.0)
            nc.vector.memset(denseT[:, :], 1.0).then_inc(s_w1s, 1)
            dve.wait_ge(s_w1s, 2)
            for u in range(2):
                for q in range(QUADS):
                    last = nc.vector.memset(diag[q * K:(q + 1) * K, u, :, q, FIELDS], 1.0)
            dve.wait_ge(s_w1, 48)
            nc.vector.tensor_scalar(bias_z[:, :], bias_in[:, :], float(K), None, ALU.mult).then_inc(s_w1s, 1)
            pairs = w1s[:, 0:2 * ROWS].rearrange("m (c r) -> m c r", c=2)[:, :, LIN:ROWS].rearrange(
                "m c (d i) -> m d c i", d=ND)
            for c in range(2):
                for d in range(ND):
                    for i0, i1 in ((0, C - d), (C - d, C)):
                        if i0 == i1:
                            continue
                        j0 = (i0 + d) % C
                        n = i1 - i0
                        whole = w1_sb[:, :, :].rearrange("m i j -> m (i j)")
                        a = (c * C + i0) * FIELDS + c * C + j0
                        b = (c * C + j0) * FIELDS + c * C + i0
                        ij = whole[:, a:a + (n - 1) * (FIELDS + 1) + 1:FIELDS + 1]
                        ji = whole[:, b:b + (n - 1) * (FIELDS + 1) + 1:FIELDS + 1]
                        dst = pairs[:, d, c, i0:i1]
                        if d == 0:
                            nc.vector.tensor_copy(dst, ij)
                        else:
                            nc.vector.tensor_tensor(dst, ij, ji, ALU.add)
                x = slice(c * C, (c + 1) * C)
                y = slice((1 - c) * C, (2 - c) * C)
                nc.vector.tensor_tensor(cross[:, c, WRAP:WRAP + C, :], w1_sb[:, x, y],
                                        w1_sb[:, y, x].rearrange("m j i -> m i j"), ALU.add).then_inc(s_w1s, 1)
            nc.vector.tensor_copy(w1s[:, 2 * ROWS:CW], bias_in[:, 0:1]).then_inc(s_w1s, 1)
            dve.wait_ge(s_w1s, 5)
            for c in range(2):
                nc.vector.tensor_copy(cross[:, c, 0:WRAP, :], cross[:, c, C:C + WRAP, :])
                nc.vector.tensor_copy(cross[:, c, WRAP + C:EXT, :], cross[:, c, WRAP:2 * WRAP, :]).then_inc(s_w1s, 1)
            dve.wait_ge(s_dense_pe, 1)
            nc.vector.tensor_copy(denseT[0:DENSE, :], y_ps[0:DENSE, 0:BATCH]).then_inc(s_denseT, 1)

            def transpose_fields(t):
                dve.wait_ge(s_rows[t], 16 * FIELDS)
                if t == 1:
                    dve.wait_ge(s_other_pe, len(other_banks))
                if t >= 2:
                    dve.wait_ge(s_mom_pe, 2 * GROUPS * (t - 1))
                    dve.wait_ge(s_diag, QUADS * (t - 1))
                for c in range(2):
                    last = nc.vector.transpose(feat[:, t % 2, c, 0:C, :].rearrange("p i b -> p (i b)"),
                                               rows_sb[:, t, c * C * K:(c + 1) * C * K])
                last.then_inc(s_fieldsT, 1)
                dve.wait_ge(s_fieldsT, t + 1)
                nc.vector.tensor_copy(feat[:, t % 2, :, C:LIN, :], feat[:, t % 2, :, 0:WRAP, :]).then_inc(s_wrap, 1)
                dve.wait_ge(s_wrap, t + 1)
                for c in range(2):
                    f = feat[:, t % 2, c].rearrange("p r b -> p (r b)")
                    one = f[:, 0:C * BL].unsqueeze(1).to_broadcast([P, ND, C * BL])
                    dst = f[:, LIN * BL:ROWS * BL].rearrange("p (d ib) -> p d ib", d=ND)
                    win = f[:, 0:C * BL].unsqueeze(1)
                    two = bass.AP(win.tensor, win.offset, [list(win.ap[0]), [BL, ND], [1, C * BL]])
                    nc.vector.tensor_tensor(dst, one, two, ALU.mult).then_inc(s_pairs, 1)

            def relu1(t):
                dve.wait_ge(s_h1_pe, t + 1)
                if t >= 1:
                    dve.wait_ge(s_h2_pe, t)
                nc.vector.tensor_scalar(h1_sb[:, :], h1_ps[:, 0:MID1 * P], 0.0, None, ALU.max).then_inc(s_h1, 1)

            def relu2(t):
                dve.wait_ge(s_h2_pe, t + 1)
                if t >= 1:
                    dve.wait_ge(s_y_pe, t)
                for m in range(MID2):
                    nc.vector.tensor_scalar(h2_sb[:, m, :], h2_ps[:, m * P:(m + 1) * P], bt2[:, m:m + 1], 0.0,
                                            ALU.add, ALU.max).then_inc(s_h2, 1)

            for n, fs in enumerate(other_banks):
                dve.wait_ge(s_other_pe, n + 1)
                if n == 0:
                    dve.wait_ge(s_own, len(own_banks))
                for k, f in enumerate(fs):
                    c, a = divmod(f, C)
                    got = ring[n % 4][:, k * CROSS:(k + 1) * CROSS].rearrange("h (u l) -> h u l", u=C)
                    ls = slice((1 - c) * C, (2 - c) * C)
                    table = coef[:, ls, c * ROWS + LIN:(c + 1) * ROWS].rearrange("h l r -> h r l")
                    parts = [(table[:, a:a + C * (ND - 1) + 1:C, :], got[:, WRAP:, :])]
                    down = min(WRAP, a)
                    if down:
                        r0 = (C - 1) * 1 + a
                        parts.append((table[:, r0:r0 + (C - 1) * (down - 1) + 1:C - 1, :],
                                      got[:, WRAP - 1 - (down - 1):WRAP, :][:, ::-1, :]))
                    if down < WRAP:
                        r0 = (C - 1) * (down + 1) + C + a
                        cnt = WRAP - down
                        parts.append((table[:, r0:r0 + (C - 1) * (cnt - 1) + 1:C - 1, :],
                                      got[:, 0:cnt, :][:, ::-1, :]))
                    for dst, src in parts:
                        last = nc.vector.tensor_tensor(dst, dst, src, ALU.add)
                    last.then_inc(s_other, 1)
                    dve.wait_ge(s_other, f + 1)
            for c in range(2):
                last = nc.vector.tensor_copy(bsum[:, c, 0:C], coef[:, c * C:(c + 1) * C, 2 * ROWS])
            last.then_inc(s_bsum, 1)
            transpose_fields(0)
            for n, (group, dst) in enumerate(turn_banks):
                if n % 2 == 1:
                    dve.wait_ge(s_ct_pe, n + 1)
                    nc.vector.tensor_copy(dst, ring[n % 4][0:group[0][1], 0:len(group) * P]).then_inc(s_ct_dve, 1)
            for t in range(1, TILES):
                transpose_fields(t)
                if t == 1:
                    dve.wait_ge(s_top, 96)
                relu1(t - 1)
                relu2(t - 1)
            relu1(TILES - 1)
            relu2(TILES - 1)
            dve.wait_ge(s_y_pe, TILES)
            nc.vector.tensor_copy(y_sb[:, :], y_ps[0:1, 0:BATCH]).then_inc(s_y, 1)

        @block.tensor
        def _(pe):
            pe.wait_ge(s_zero, 2)
            pe.wait_ge(s_w2, 16)
            for n in range(BANKS_W2T):
                if n >= 4:
                    pe.wait_ge(s_w2T, n - 3)
                for k, f in enumerate(range(n * PER_BANK, min((n + 1) * PER_BANK, FIELDS))):
                    last = nc.tensor.transpose(ring[n % 4][:, k * P:(k + 1) * P], w2_nat[:, :, f], ident[:, :])
                last.then_inc(s_w2T_pe, 1)
            pe.wait_ge(s_dense, 16)
            for t in range(TILES):
                last = nc.tensor.transpose(y_ps[0:DENSE, t * P:(t + 1) * P], dense_sb[:, t, :], ident[:, :])
            last.then_inc(s_dense_pe, 1)
            pe.wait_ge(s_w2T, BANKS_W2T)
            pe.wait_ge(s_w1s, 6)
            for n, fs in enumerate(own_banks):
                if n >= 4:
                    pe.wait_ge(s_own, n - 3)
                for k, f in enumerate(fs):
                    last = nc.tensor.matmul(ring[n % 4][:, k * CW:(k + 1) * CW], w2T[:, f, :], w1s[:, :],
                                            start=True, stop=True)
                last.then_inc(s_own_pe, 1)
            pe.wait_ge(s_own, len(own_banks))
            pe.wait_ge(s_w1s, 8)
            for n, fs in enumerate(other_banks):
                if n >= 4:
                    pe.wait_ge(s_other, OTHER_PER_BANK * (n - 3))
                for k, f in enumerate(fs):
                    c, a = divmod(f, C)
                    last = nc.tensor.matmul(ring[n % 4][:, k * CROSS:(k + 1) * CROSS], w2T[:, f, :],
                                            cross[:, c, a:a + C, :].rearrange("m x l -> m (x l)"),
                                            start=True, stop=True)
                last.then_inc(s_other_pe, 1)
            pe.wait_ge(s_other, FIELDS)

            def moments(t):
                pe.wait_ge(s_diag, QUADS * (t + 1))
                for n in range(2 * GROUPS):
                    c, g = divmod(n, GROUPS)
                    pe.wait_ge(s_pairs, 2 * t + c + 1)
                    if n >= 4 or t >= 1:
                        pe.wait_ge(s_mom, 2 * GROUPS * t + n - 3)
                    for b in range(GROUP):
                        s = g * GROUP + b
                        last = nc.tensor.matmul(ring[n % 4][0:ROWS, b * QUADS * COLS:(b + 1) * QUADS * COLS],
                                                feat[:, t % 2, c, :, s],
                                                diag[:, t % 2, s].rearrange("p q l -> p (q l)"),
                                                start=True, stop=True)
                    last.then_inc(s_mom_pe, 1)

            def contract(t):
                pe.wait_ge(s_mom, 2 * GROUPS * (t + 1))
                if t >= 1:
                    pe.wait_ge(s_z, 2 * t)
                z1 = [(w1T[:, c, :], mom[:, FIELDS, c, :]) for c in range(2)]
                z1 += [(crossT[:, l, :], mom[0:C, C + l, 0, :]) for l in range(C)]
                z2 = [(bsumT[:, c, :], mom[:, FIELDS, c, :]) for c in range(2)]
                z2 += [(coefT[:, l, c, :], mom[:, l, c, :]) for l in range(FIELDS) for c in range(2)]
                for n, terms in enumerate((z1, z2)):
                    for k, (w, m) in enumerate(terms):
                        last = nc.tensor.matmul(z_ps[:, n * P:(n + 1) * P], w, m,
                                                start=(k == 0), stop=(k == len(terms) - 1))
                last.then_inc(s_z_pe, 1)

            def mlp(t):
                if t == 0:
                    pe.wait_ge(s_top, 96)
                    pe.wait_ge(s_denseT, 1)
                pe.wait_ge(s_z, 2 * (t + 1))
                if t >= 1:
                    pe.wait_ge(s_h1, t)
                for m in range(MID1):
                    terms = [(wt1[:, n, m * P:(m + 1) * P], z_sb[:, n, :]) for n in range(2)]
                    terms.append((wt1d[:, m * P:(m + 1) * P], denseT[0:DENSE + 1, t * P:(t + 1) * P]))
                    for k, (w, x) in enumerate(terms):
                        last = nc.tensor.matmul(h1_ps[:, m * P:(m + 1) * P], w, x, start=(k == 0), stop=(k == 2))
                last.then_inc(s_h1_pe, 1)
                pe.wait_ge(s_h1, t + 1)
                if t >= 1:
                    pe.wait_ge(s_h2, MID2 * t)
                for m in range(MID2):
                    for k in range(MID1):
                        last = nc.tensor.matmul(h2_ps[:, m * P:(m + 1) * P], wt2[:, k, m * P:(m + 1) * P],
                                                h1_sb[:, k * P:(k + 1) * P], start=(k == 0), stop=(k == MID1 - 1))
                last.then_inc(s_h2_pe, 1)
                pe.wait_ge(s_h2, MID2 * (t + 1))
                for m in range(MID2):
                    last = nc.tensor.matmul(y_ps[0:1, t * P:(t + 1) * P], wt3[:, m:m + 1], h2_sb[:, m, :],
                                            start=(m == 0), stop=(m == MID2 - 1))
                last.then_inc(s_y_pe, 1)

            moments(0)
            pe.wait_ge(s_mom, 2 * GROUPS)
            pe.wait_ge(s_bsum, 1)
            for n, (group, dst) in enumerate(turn_banks):
                if n >= 4:
                    pe.wait_ge(s_ct_act if n % 2 == 0 else s_ct_dve, (n - 4) // 2 + 1)
                for k, (src, rows, _) in enumerate(group):
                    last = nc.tensor.transpose(ring[n % 4][0:rows, k * P:(k + 1) * P], src, ident[:, :])
                last.then_inc(s_ct_pe, 1)
            turned(pe, len(turn_banks))
            contract(0)
            for t in range(1, TILES):
                moments(t)
                mlp(t - 1)
                contract(t)
            mlp(TILES - 1)


_TABLES = [f"tbl_{i}" for i in range(26)]
_INS = ["dense_ctx", "ids", *_TABLES, "W_top1", "b_top1", "W_top2", "b_top2", "W_top3",
        "L0_rec_W1", "L0_rec_b1", "L0_rec_W2", "L0_rec_b2"]


def kernel(**inputs):
    import numpy as _np
    import concourse.bacc as _bacc
    from concourse import mybir as _mybir
    from concourse.bass_utils import run_bass_kernel_spmd as _run

    nc = _bacc.Bacc("TRN2", target_bir_lowering=False, num_devices=1)
    arrays, args = {}, {}
    for name in _INS:
        a = _np.ascontiguousarray(inputs[name])
        arrays[f"in_{name}_dram"] = a
        args[name] = nc.dram_tensor(f"in_{name}_dram", a.shape, _mybir.dt.from_np(a.dtype), kind="ExternalInput").ap()
    batch = inputs["ids"].shape[0]
    out = nc.dram_tensor("out_0_dram", (batch, 1), _mybir.dt.float32, kind="ExternalOutput").ap()
    dlrm_cin_tower(nc, args["dense_ctx"], args["ids"], [args[n] for n in _TABLES], args["W_top1"], args["b_top1"],
                   args["W_top2"], args["b_top2"], args["W_top3"], args["L0_rec_W1"], args["L0_rec_b1"],
                   args["L0_rec_W2"], args["L0_rec_b2"], out)
    r = _run(nc, [arrays], core_ids=[0])
    return r.results[0]["out_0_dram"]
```

```python
from contextlib import ExitStack

import concourse.bass as bass
from concourse import mybir

F32 = mybir.dt.float32
U32 = mybir.dt.uint32
ALU = mybir.AluOpType
ACT = mybir.ActivationFunctionType


def dlrm_cin_tower(nc, dense_ctx, ids, tables, w_top1, b_top1, w_top2, b_top2, w_top3, w1, b1, w2, b2, out):
    P = 128
    BATCH, FIELDS = ids.shape
    K = tables[0].shape[1]
    H1, H2 = w1.shape[0], w2.shape[0]
    DENSE = dense_ctx.shape[1]
    TOP1, TOP2 = w_top2.shape
    TILES = BATCH // P
    QUADS = P // K
    BL = P // QUADS
    C = FIELDS // 2
    ND = C // 2 + 1
    WRAP = ND - 1
    PAIRS = ND * C
    LIN = -(-PAIRS // 32) * 32
    ROWS = LIN + C
    HALF = P // 2
    COLS = FIELDS + 1
    GROUP = 4
    GROUPS = BL // GROUP
    EXT = 2 * C - 1
    CW = 2 * PAIRS + 1
    XG = -(-C // QUADS)
    MID1 = TOP1 // P
    MID2 = TOP2 // P
    CROSS = C * C
    PER_BANK = 512 // P
    assert (P, K, H1, H2) == (128, 32, 128, 128) and FIELDS == 2 * C and C % 2 == 1 and ROWS <= P

    with ExitStack() as ctx:
        def sb(name, shape, dt=F32):
            return ctx.enter_context(nc.sbuf_tensor(name, shape, dt))

        def bank(name):
            return ctx.enter_context(nc.psum_tensor(name, [P, 512], F32))

        def sem(name):
            return ctx.enter_context(nc.semaphore(name))

        ids_sb = sb("ids_sb", [P, TILES, FIELDS], U32)
        rows_sb = sb("rows_sb", [P, TILES, FIELDS * K])
        feat = sb("feat", [P, 2, 2, ROWS + WRAP, BL])
        diag = sb("diag", [P, 2, BL, QUADS, COLS])
        mom_x = sb("mom_x", [ROWS, 2, C + 1, P])
        mom_s = sb("mom_s", [P, C, P])
        mom_l = sb("mom_l", [P, XG, P])
        coef = sb("coef", [P, FIELDS, CW])
        stack = sb("stack", [P, C, 2, HALF])
        coef_x = sb("coef_x", [PAIRS, 2, C, P])
        coef_s = sb("coef_s", [P, C, P])
        startup = feat[:, 1].rearrange("p c r b -> p (c r b)")
        w2_nat = startup[:, 0:H1 * FIELDS].rearrange("h (m l) -> h m l", l=FIELDS)
        w2T = startup[:, H1 * FIELDS:2 * H1 * FIELDS].rearrange("m (l h) -> m l h", l=FIELDS)
        w1_sb = sb("w1_sb", [P, FIELDS, FIELDS])
        w1s = sb("w1s", [P, CW])
        cross = sb("cross", [P, 2, EXT, C])
        cross_l = sb("cross_l", [P, XG * QUADS, 32])
        bsum = sb("bsum", [P, P])
        bsumT = sb("bsumT", [P, P])
        w1T = sb("w1T", [PAIRS, 2, P])
        crossT = sb("crossT", [P, XG, P])
        ident = sb("ident", [P, P])
        bias_in = sb("bias_in", [P, 2])
        bias_z = sb("bias_z", [P, 2])
        dense_sb = sb("dense_sb", [P, TILES, DENSE])
        denseT = sb("denseT", [32, BATCH])
        wt1 = sb("wt1", [P, 2, TOP1])
        wt1d = sb("wt1d", [DENSE + 1, TOP1])
        wt2 = sb("wt2", [P, MID1, TOP2])
        wt3 = sb("wt3", [P, MID2])
        bt2 = sb("bt2", [P, MID2])
        z_sb = sb("z_sb", [P, 2, P])
        h1_sb = sb("h1_sb", [P, MID1 * P])
        h2_sb = sb("h2_sb", [P, MID2, P])
        y_sb = sb("y_sb", [1, BATCH])

        ring = [bank(f"ring{i}") for i in range(4)]
        z_ps = [bank(f"z{n + 1}_ps") for n in range(2)]
        h1_ps = bank("h1_ps")
        h2_ps = bank("h2_ps")
        y_ps = h2_ps[0:1, MID2 * P:(MID2 + 1) * P]

        s_ids = sem("s_ids")
        s_w1 = sem("s_w1")
        s_w2 = sem("s_w2")
        s_dense = sem("s_dense")
        s_top = sem("s_top")
        s_rows = [[sem(f"s_rows{t}{x}") for x in "AB"] for t in range(TILES)]
        s_zero = sem("s_zero")
        s_clear = sem("s_clear")
        s_w1s = sem("s_w1s")
        s_w2T_pe = sem("s_w2T_pe")
        s_w2T = sem("s_w2T")
        s_own_pe = sem("s_own_pe")
        s_own = sem("s_own")
        s_other_pe = sem("s_other_pe")
        s_other = sem("s_other")
        s_bsum = sem("s_bsum")
        s_fold = sem("s_fold")
        s_gap = sem("s_gap")
        s_lin = sem("s_lin")
        s_ct_pe = sem("s_ct_pe")
        s_ct_act = sem("s_ct_act")
        s_ct_dve = sem("s_ct_dve")
        s_dense_pe = sem("s_dense_pe")
        s_denseT = sem("s_denseT")
        s_fieldsT = sem("s_fieldsT")
        s_wrap = sem("s_wrap")
        s_pairs = sem("s_pairs")
        s_diag = sem("s_diag")
        s_mom_pe = sem("s_mom_pe")
        s_mom = sem("s_mom")
        s_z1_pe = sem("s_z1_pe")
        s_z_pe = sem("s_z_pe")
        s_z = sem("s_z")
        s_h1_pe = sem("s_h1_pe")
        s_h1 = sem("s_h1")
        s_h2_pe = sem("s_h2_pe")
        s_h2 = sem("s_h2")
        s_y_pe = sem("s_y_pe")
        s_y = sem("s_y")
        s_out = sem("s_out")

        BANKS_W2T = -(-FIELDS // PER_BANK)
        OWN_PER_BANK = 2
        WARM = 24
        OTHER_PER_BANK = 3
        own_banks = [range(f, min(f + OWN_PER_BANK, FIELDS)) for f in range(0, FIELDS, OWN_PER_BANK)]
        in_turn = [c * C + a for a in range(C) for c in range(2)]
        other_banks = [in_turn[n:n + OTHER_PER_BANK] for n in range(0, FIELDS, OTHER_PER_BANK)]

        flat = lambda ap: ap.rearrange("r l h -> r (l h)")
        turn_banks = []
        turn_banks.append(([w1s[:, c * PAIRS:(c + 1) * PAIRS] for c in range(2)], PAIRS, flat(w1T[:, :, :])))
        turn_banks.append(([cross_l[:, g * QUADS:(g + 1) * QUADS, :].rearrange("m j i -> m (j i)")
                            for g in range(XG)], P, flat(crossT[:, :, :])))
        for c in range(2):
            for l0 in range(0, C, PER_BANK):
                l1 = min(l0 + PER_BANK, C)
                turn_banks.append(([coef[:, (1 - c) * C + l, c * PAIRS:(c + 1) * PAIRS] for l in range(l0, l1)], PAIRS,
                                   flat(coef_x[:, c, l0:l1, :])))
        for l0 in range(0, C, PER_BANK):
            l1 = min(l0 + PER_BANK, C)
            turn_banks.append(([stack[:, l].rearrange("h c r -> h (c r)") for l in range(l0, l1)], P,
                               flat(coef_s[:, l0:l1, :])))
        turn_banks.append(([bsum[:, :]], P, bsumT[:, :]))

        folds = []
        def other_name(d, s):
            down, up = (s, d - s) if s <= d else (C - s, s - d)
            if s <= d:
                names = [(down, 0, d), (up, s, 0)]
            else:
                names = [(up, d, 0), (down, s, d)]
            return sorted(names, key=lambda n: n[0])
        for d in range(HALF // C, ND):
            for s in range(C):
                for i in range(C):
                    if d * C + i < HALF:
                        continue
                    d2, shift, l_shift = next(n for n in other_name(d, s) if n[0] * C + (i + n[1]) % C < HALF)
                    folds.append((d, s, i, d2, (i + shift) % C, (i + l_shift) % C))
        fold_runs = {}
        for d, s, i, d2, i2, l2 in folds:
            src, dst = ((i + s) % C, d * C + i), (l2, d2 * C + i2)
            runs = fold_runs.setdefault((d2, (l2 - i2) % C), {}).setdefault((d, s), [])
            if runs:
                s0, t0, n = runs[-1]
                if src == (s0[0] + n, s0[1] + n) and dst == (t0[0] + n, t0[1] + n):
                    runs[-1] = (s0, t0, n + 1)
                    continue
            runs.append((src, dst, 1))
        fold_rounds = []
        for by_source in fold_runs.values():
            for n, runs in enumerate(by_source.values()):
                if n == len(fold_rounds):
                    fold_rounds.append([])
                fold_rounds[n] += runs
        FOLDS = 1 + len(fold_rounds)

        MOM_BANKS = 2 * GROUPS

        FIRST = 2
        EARLY = FIRST + 4
        LATE = FIRST + 2 * -(-C // PER_BANK)
        spare = [h1_ps, h2_ps, z_ps[0], z_ps[1]]
        turn_ps = [spare[n % 4] if n < LATE else ring[n % 4] for n in range(len(turn_banks))]
        on_act = [n < EARLY or (n >= LATE and n % 2 == 0) for n in range(len(turn_banks))]

        def turned(eng, upto):
            eng.wait_ge(s_ct_act, sum(on_act[:upto]))
            if upto > sum(on_act[:upto]):
                eng.wait_ge(s_ct_dve, upto - sum(on_act[:upto]))

        block = ctx.enter_context(nc.Block())

        @block.sync
        def _(sp):
            sp.dma_start(ids_sb[:, :, :], ids.bitcast(U32).rearrange("(t p) f -> p t f", p=P)).then_inc(s_ids, 16)
            sp.dma_start(w1_sb[:, :, :], w1).then_inc(s_w1, 16)
            with nc.allow_non_contiguous_dma(reason="a few hundred biases"):
                sp.dma_start(bias_in[:, 0:1], b1.rearrange("(p a) -> p a", a=1)).then_inc(s_w1, 16)
                sp.dma_start(bias_in[:, 1:2], b2.rearrange("(p a) -> p a", a=1)).then_inc(s_w1, 16)
                sp.dma_start(w2_nat, w2).then_inc(s_w2, 16)
                sp.dma_start(dense_sb[:, :, :], dense_ctx.rearrange("(t p) f -> p t f", p=P)).then_inc(s_dense, 16)
                sp.dma_start(wt1[:, :, :], w_top1[0:2 * P, :].rearrange("(c p) n -> p c n", p=P)).then_inc(s_top, 16)
                sp.dma_start(wt1d[0:DENSE, :], w_top1[2 * P:2 * P + DENSE, :]).then_inc(s_top, 16)
                sp.dma_start(wt1d[DENSE:DENSE + 1, :], b_top1.rearrange("(a n) -> a n", a=1)).then_inc(s_top, 16)
                sp.dma_start(wt2[:, :, :], w_top2.rearrange("(c p) n -> p c n", p=P)).then_inc(s_top, 16)
                sp.dma_start(wt3[:, :], w_top3.rearrange("(c p) a -> p (c a)", p=P)).then_inc(s_top, 16)
                sp.dma_start(bt2[:, :], b_top2.rearrange("(c p) -> p c", p=P)).then_inc(s_top, 16)
            sp.wait_ge(s_y, TILES)
            sp.dma_start(out.rearrange("b a -> a b"), y_sb[:, :]).then_inc(s_out, 16)
            sp.wait_ge(s_out, 16)

        @block.gpsimd
        def _(pool):
            nc.gpsimd.memset(ident[:, :], 0.0).then_inc(s_zero, 1)
            pool.wait_ge(s_zero, 1)
            nc.gpsimd.affine_select(out=ident[:, :], in_=ident[:, :], compare_op=ALU.not_equal, fill=1.0, base=0,
                                    pattern=[[-1, P]], channel_multiplier=1).then_inc(s_zero, 1)
            pool.wait_ge(s_ids, 16)
            for t in range(TILES):
                for f in range(FIELDS):
                    nc.gpsimd.indirect_dma_start(
                        rows_sb[:, t, f * K:(f + 1) * K], None, tables[f],
                        bass.IndirectOffsetOnAxis(ap=ids_sb[:, t, f:f + 1], axis=0)).then_inc(s_rows[t][f // C], 16)

        @block.scalar
        def _(act):
            def copy_diag(t):
                if t <= 1:
                    act.wait_ge(s_clear, 2 * (t + 1))
                if t >= 2:
                    act.wait_ge(s_mom_pe, MOM_BANKS * (t - 1))
                for c in range(2):
                    act.wait_ge(s_fieldsT, 2 * t + c + 1)
                    for q in range(QUADS):
                        src = feat[q * K:(q + 1) * K, t % 2, c, LIN:ROWS, :]
                        dst = diag[q * K:(q + 1) * K, t % 2, :, q, c * C:(c + 1) * C].rearrange("p b i -> p i b")
                        nc.scalar.copy(dst, src).then_inc(s_diag, 1)

            def copy_moments(t):
                for n in range(MOM_BANKS):
                    c, g = divmod(n, GROUPS)
                    act.wait_ge(s_mom_pe, MOM_BANKS * t + n + 1)
                    if n == 0 and t >= 1:
                        act.wait_ge(s_z_pe, t)
                        act.wait_ge(s_lin, 2 * t)
                    src = ring[n % 4][:, 0:GROUP * QUADS * COLS].rearrange("r (b q l) -> r b q l", b=GROUP, q=QUADS)
                    samples = lambda ap: ap.rearrange("r l (q g b) -> r g b q l", q=QUADS, b=GROUP)[:, g]
                    if c == 0:
                        nc.scalar.copy(samples(mom_x[:, 0]), src[0:ROWS, :, :, C:COLS])
                    else:
                        nc.scalar.copy(samples(mom_x[:, 1, 0:C]), src[0:ROWS, :, :, 0:C])
                        nc.scalar.copy(samples(mom_x[:, 1, C:C + 1]), src[0:ROWS, :, :, FIELDS:COLS])
                    nc.scalar.copy(samples(mom_s[c * HALF:(c + 1) * HALF]),
                                   src[0:HALF, :, :, c * C:(c + 1) * C]).then_inc(s_mom, 1)

            def copy_z(t):
                if t >= 1:
                    act.wait_ge(s_h1_pe, MID1 * t)
                for n in range(2):
                    act.wait_ge(s_z1_pe if n == 0 else s_z_pe, t + 1)
                    nc.scalar.activation(z_sb[:, n, :], z_ps[n][:, 0:P], ACT.Identity,
                                         bias=bias_z[:, n:n + 1]).then_inc(s_z, 1)

            def copy_turned(first, end):
                for n in range(first, end):
                    group, rows, dst = turn_banks[n]
                    if on_act[n]:
                        act.wait_ge(s_ct_pe, n + 1)
                        nc.scalar.copy(dst, turn_ps[n][0:rows, 0:len(group) * P]).then_inc(s_ct_act, 1)

            for n in range(BANKS_W2T):
                f0, f1 = n * PER_BANK, min((n + 1) * PER_BANK, FIELDS)
                act.wait_ge(s_w2T_pe, n + 1)
                nc.scalar.copy(w2T[:, f0:f1, :].rearrange("m l h -> m (l h)"),
                               ring[n % 4][:, 0:(f1 - f0) * P]).then_inc(s_w2T, 1)
            for n, fs in enumerate(own_banks):
                act.wait_ge(s_own_pe, n + 1)
                nc.scalar.copy(coef[:, fs[0]:fs[-1] + 1, :].rearrange("h l r -> h (l r)"),
                               ring[n % 4][:, 0:len(fs) * CW]).then_inc(s_own, 1)
            copy_turned(0, FIRST)
            copy_diag(0)
            copy_turned(FIRST, EARLY)
            copy_moments(0)
            copy_turned(LATE, len(turn_banks))
            for t in range(1, TILES):
                copy_diag(t)
                if t == 1:
                    act.wait_ge(s_w1s, 1)
                copy_z(t - 1)
                copy_moments(t)
            copy_z(TILES - 1)

        @block.vector
        def _(dve):
            def clear_diag(u):
                nc.vector.memset(diag[:, u].rearrange("p b q l -> p (b q l)"), 0.0).then_inc(s_clear, 1)
                dve.wait_ge(s_clear, 2 * u + 1)
                for q in range(QUADS):
                    last = nc.vector.memset(diag[q * K:(q + 1) * K, u, :, q, FIELDS], 1.0)
                last.then_inc(s_clear, 1)

            clear_diag(0)
            dve.wait_ge(s_w1, 48)
            nc.vector.tensor_scalar(bias_z[:, :], bias_in[:, :], float(K), None, ALU.mult).then_inc(s_w1s, 1)
            whole = w1_sb[:, :, :].rearrange("m i j -> m (i j)")
            clique_step = C * (FIELDS + 1)

            def diagonal(i0, j0, n):
                at = whole[:, i0 * FIELDS + j0:].unsqueeze(1)
                return bass.AP(at.tensor, at.offset, [list(at.ap[0]), [clique_step, 2], [FIELDS + 1, n]])

            for d in range(ND):
                for i0, i1 in ((0, C - d), (C - d, C)):
                    if i0 == i1:
                        continue
                    j0 = (i0 + d) % C
                    dst = w1s[:, 0:2 * PAIRS].rearrange("m (c r) -> m c r", c=2)[:, :, d * C + i0:d * C + i1]
                    if d == 0:
                        nc.vector.tensor_copy(dst, diagonal(i0, j0, i1 - i0))
                    else:
                        nc.vector.tensor_tensor(dst, diagonal(i0, j0, i1 - i0), diagonal(j0, i0, i1 - i0), ALU.add)
            nc.vector.tensor_copy(w1s[:, 2 * PAIRS:CW], bias_in[:, 0:1]).then_inc(s_w1s, 1)
            for c in range(2):
                x = slice(c * C, (c + 1) * C)
                y = slice((1 - c) * C, (2 - c) * C)
                nc.vector.tensor_tensor(cross[:, c, WRAP:WRAP + C, :], w1_sb[:, x, y],
                                        w1_sb[:, y, x].rearrange("m j i -> m i j"), ALU.add).then_inc(s_w1s, 1)
            dve.wait_ge(s_w1s, 4)
            for c in range(2):
                nc.vector.tensor_copy(cross[:, c, 0:WRAP, :], cross[:, c, C:C + WRAP, :])
                nc.vector.tensor_copy(cross[:, c, WRAP + C:EXT, :], cross[:, c, WRAP:2 * WRAP, :]).then_inc(s_w1s, 1)
            nc.vector.memset(cross_l[:, :, :], 0.0)
            nc.vector.memset(bsum[:, :], 0.0)
            nc.vector.memset(mom_l[:, :, :], 0.0)
            nc.vector.memset(denseT[:, :], 1.0).then_inc(s_w1s, 1)
            nc.vector.memset(feat[:, 0, :, PAIRS:LIN, :], 0.0).then_inc(s_gap, 1)
            dve.wait_ge(s_w1s, 7)
            nc.vector.tensor_copy(cross_l[:, 0:C, 0:C], cross[:, 0, WRAP:WRAP + C, :].rearrange("m i l -> m l i"))
            clear_diag(1)
            dve.wait_ge(s_dense_pe, 1)
            nc.vector.tensor_copy(denseT[0:DENSE, :], h1_ps[0:DENSE, 0:BATCH]).then_inc(s_denseT, 1)

            def pair_rows(t, c):
                return feat[:, t % 2, c].rearrange("p r b -> p (r b)")

            def fields_of(t, c):
                if t == 1 and c == 0:
                    dve.wait_ge(s_other_pe, len(other_banks))
                    nc.vector.memset(feat[:, 1, :, PAIRS:LIN, :], 0.0).then_inc(s_gap, 1)
                if t >= 2 and c == 0:
                    dve.wait_ge(s_mom_pe, MOM_BANKS * (t - 1))
                    dve.wait_ge(s_diag, 2 * QUADS * (t - 1))
                f = pair_rows(t, c)
                dve.wait_ge(s_rows[t][c], 16 * C)
                nc.vector.transpose(f[:, LIN * BL:ROWS * BL],
                                    rows_sb[:, t, c * C * K:(c + 1) * C * K]).then_inc(s_fieldsT, 1)

            def products_of(t, c):
                f = pair_rows(t, c)
                dve.wait_ge(s_fieldsT, 2 * t + c + 1)
                nc.vector.tensor_copy(f[:, ROWS * BL:(ROWS + WRAP) * BL],
                                      f[:, LIN * BL:(LIN + WRAP) * BL]).then_inc(s_wrap, 1)
                dve.wait_ge(s_wrap, 2 * t + c + 1)
                one = f[:, LIN * BL:ROWS * BL].unsqueeze(1)
                two = bass.AP(one.tensor, one.offset, [list(one.ap[0]), [BL, ND], [1, C * BL]])
                dst = f[:, 0:PAIRS * BL].rearrange("p (d ib) -> p d ib", d=ND)
                nc.vector.tensor_tensor(dst, one.to_broadcast([P, ND, C * BL]), two, ALU.mult).then_inc(s_pairs, 1)

            def fields(t):
                for c in range(2):
                    fields_of(t, c)

            def products(t):
                for c in range(2):
                    products_of(t, c)

            def copy_lin(t):
                for c in range(2):
                    dve.wait_ge(s_mom, MOM_BANKS * (t + 1) - GROUPS * (1 - c))
                    if t >= 1 and c == 0:
                        dve.wait_ge(s_z_pe, t)
                    if c == 0:
                        for j in range(QUADS):
                            n = len(range(j, C, QUADS))
                            nc.vector.tensor_copy(mom_l[32 * j:32 * j + C, 0:n, :], mom_x[LIN:ROWS, 0, j:C:QUADS, :])
                    q = 32 * (1 + c)
                    nc.vector.tensor_copy(mom_l[q:q + C, XG - 1, :], mom_x[LIN:ROWS, c, C, :]).then_inc(s_lin, 1)

            def relu1(t):
                for m in range(MID1):
                    dve.wait_ge(s_h1_pe, MID1 * (t + 1))
                    if t >= 1 and m == 0:
                        dve.wait_ge(s_h2_pe, t)
                    nc.vector.tensor_scalar(h1_sb[:, m * P:(m + 1) * P], h1_ps[:, m * P:(m + 1) * P], 0.0, None,
                                            ALU.max).then_inc(s_h1, 1)

            def relu2(t):
                dve.wait_ge(s_h2_pe, t + 1)
                if t >= 1:
                    dve.wait_ge(s_y_pe, t)
                for m in range(MID2):
                    nc.vector.tensor_scalar(h2_sb[:, m, :], h2_ps[:, m * P:(m + 1) * P], bt2[:, m:m + 1], 0.0,
                                            ALU.add, ALU.max).then_inc(s_h2, 1)

            done = 0
            for n, fs in enumerate(other_banks):
                dve.wait_ge(s_other_pe, n + 1)
                if n == 0:
                    dve.wait_ge(s_own, len(own_banks))
                for k, f in enumerate(fs):
                    c, a = divmod(f, C)
                    got = ring[(len(own_banks) + n) % 4][:, k * CROSS:(k + 1) * CROSS].rearrange("h (u l) -> h u l", u=C)
                    ls = slice((1 - c) * C, (2 - c) * C)
                    table = coef[:, ls, c * PAIRS:(c + 1) * PAIRS].rearrange("h l r -> h r l")
                    if done >= 2:
                        dve.wait_ge(s_other, done - 1)
                    parts = [(table[:, a:a + C * (ND - 1) + 1:C, :], got[:, WRAP:, :])]
                    down = min(WRAP, a)
                    if down:
                        r0 = (C - 1) * 1 + a
                        parts.append((table[:, r0:r0 + (C - 1) * (down - 1) + 1:C - 1, :],
                                      got[:, WRAP - 1 - (down - 1):WRAP, :][:, ::-1, :]))
                    if down < WRAP:
                        r0 = (C - 1) * (down + 1) + C + a
                        cnt = WRAP - down
                        parts.append((table[:, r0:r0 + (C - 1) * (cnt - 1) + 1:C - 1, :],
                                      got[:, 0:cnt, :][:, ::-1, :]))
                    for dst, src in parts:
                        last = nc.vector.tensor_tensor(dst, dst, src, ALU.add)
                    last.then_inc(s_other, 1)
                    done += 1

            def copy_turned(first, end):
                for n in range(first, end):
                    group, rows, dst = turn_banks[n]
                    if not on_act[n]:
                        dve.wait_ge(s_ct_pe, n + 1)
                        nc.vector.tensor_copy(dst, turn_ps[n][0:rows, 0:len(group) * P]).then_inc(s_ct_dve, 1)

            fields(0)
            products(0)
            copy_turned(EARLY, LATE)
            for c in range(2):
                q = 32 * (1 + c)
                last = nc.vector.tensor_copy(bsum[:, q:q + C], coef[:, c * C:(c + 1) * C, 2 * PAIRS])
            last.then_inc(s_bsum, 1)

            def steps(ap, clique_step, step, n):
                return bass.AP(ap.tensor, ap.offset, [list(ap.ap[0]), [clique_step, 2], [step, n]])

            def fold():
                rows = lambda c: coef[:, c * C:(c + 1) * C, c * PAIRS:c * PAIRS + HALF]
                for c in range(2):
                    last = nc.vector.tensor_copy(stack[:, :, c, :], rows(c))
                last.then_inc(s_fold, 1)
                dve.wait_ge(s_fold, 1)
                for n, runs in enumerate(fold_rounds):
                    if n >= 1:
                        dve.wait_ge(s_fold, n + 1)
                    for (l1, r1), (l2, r2), count in runs:
                        dst = steps(stack[:, l2, 0, r2:], HALF, 2 * HALF + 1, count)
                        src = steps(coef[:, l1, r1:], C * CW + PAIRS, CW + 1, count)
                        last = nc.vector.tensor_tensor(dst, dst, src, ALU.add)
                    last.then_inc(s_fold, 1)

            fold()
            copy_lin(0)
            copy_turned(LATE, len(turn_banks))

            def finish(t):
                relu1(t)
                relu2(t)
                dve.wait_ge(s_y_pe, t + 1)
                nc.vector.tensor_copy(y_sb[:, t * P:(t + 1) * P], y_ps).then_inc(s_y, 1)

            for t in range(1, TILES):
                fields(t)
                products(t)
                if t == 1:
                    dve.wait_ge(s_top, 96)
                finish(t - 1)
                copy_lin(t)
            finish(TILES - 1)

        @block.tensor
        def _(pe):
            pe.wait_ge(s_zero, 2)
            for n in range(WARM):
                nc.tensor.matmul(z_ps[0][:, 0:P], ident[:, :], ident[:, :], start=True, stop=True)
            pe.wait_ge(s_w2, 16)
            for n in range(BANKS_W2T):
                if n >= 4:
                    pe.wait_ge(s_w2T, n - 3)
                for k, f in enumerate(range(n * PER_BANK, min((n + 1) * PER_BANK, FIELDS))):
                    last = nc.tensor.transpose(ring[n % 4][:, k * P:(k + 1) * P], w2_nat[:, :, f], ident[:, :])
                last.then_inc(s_w2T_pe, 1)
            pe.wait_ge(s_dense, 16)
            for t in range(TILES):
                last = nc.tensor.transpose(h1_ps[0:DENSE, t * P:(t + 1) * P], dense_sb[:, t, :], ident[:, :])
            last.then_inc(s_dense_pe, 1)
            pe.wait_ge(s_w1s, 2)
            for n, fs in enumerate(own_banks):
                pe.wait_ge(s_w2T, min(BANKS_W2T, BANKS_W2T - 2 + n))
                if n >= 4:
                    pe.wait_ge(s_own, n - 3)
                for k, f in enumerate(fs):
                    last = nc.tensor.matmul(ring[n % 4][:, k * CW:(k + 1) * CW], w2T[:, f, :], w1s[:, :],
                                            start=True, stop=True)
                last.then_inc(s_own_pe, 1)
            pe.wait_ge(s_w1s, 6)
            for n, fs in enumerate(other_banks):
                if n < 4:
                    pe.wait_ge(s_own, len(own_banks) - 3 + n)
                else:
                    pe.wait_ge(s_other, OTHER_PER_BANK * (n - 3))
                for k, f in enumerate(fs):
                    c, a = divmod(f, C)
                    last = nc.tensor.matmul(ring[(len(own_banks) + n) % 4][:, k * CROSS:(k + 1) * CROSS], w2T[:, f, :],
                                            cross[:, c, a:a + C, :].rearrange("m x l -> m (x l)"),
                                            start=True, stop=True)
                last.then_inc(s_other_pe, 1)

            def turn(first, end):
                for n in range(first, end):
                    before = [k for k in range(n) if turn_ps[k] is turn_ps[n]]
                    if before:
                        turned(pe, before[-1] + 1)
                    for k, src in enumerate(turn_banks[n][0]):
                        last = nc.tensor.transpose(turn_ps[n][0:turn_banks[n][1], k * P:(k + 1) * P], src, ident[:, :])
                    last.then_inc(s_ct_pe, 1)

            def moments(t, between):
                if t <= 1:
                    pe.wait_ge(s_gap, t + 1)
                pe.wait_ge(s_diag, 2 * QUADS * (t + 1))
                for n in range(MOM_BANKS):
                    c, g = divmod(n, GROUPS)
                    if n in between:
                        between[n](t - 1)
                    if g == 0:
                        pe.wait_ge(s_pairs, 2 * t + c + 1)
                    if t >= 1 or n >= 4:
                        pe.wait_ge(s_mom, MOM_BANKS * t + n - 3)
                    for b in range(GROUP):
                        s = g * GROUP + b
                        last = nc.tensor.matmul(ring[n % 4][0:ROWS, b * QUADS * COLS:(b + 1) * QUADS * COLS],
                                                feat[:, t % 2, c, 0:ROWS, s],
                                                diag[:, t % 2, s].rearrange("p q l -> p (q l)"),
                                                start=True, stop=True)
                    last.then_inc(s_mom_pe, 1)

            def contract(t):
                if t >= 1:
                    pe.wait_ge(s_z, 2 * t)
                x_terms = [[(coef_x[:, c, l, :], mom_x[0:PAIRS, c, l, :]) for l in range(C)] for c in range(2)]
                s_terms = [(coef_s[:, l, :], mom_s[:, l, :]) for l in range(C)]
                z1_terms = [(w1T[:, c, :], mom_x[0:PAIRS, c, C, :]) for c in range(2)]
                z1_terms += [(crossT[:, g, :], mom_l[:, g, :]) for g in range(XG)]

                def add(n, terms, start, stop):
                    for k, (w, m) in enumerate(terms):
                        last = nc.tensor.matmul(z_ps[n][:, 0:P], w, m, start=(start and k == 0),
                                                stop=(stop and k == len(terms) - 1))
                    return last

                if t == 0:
                    turned(pe, LATE)
                pe.wait_ge(s_mom, MOM_BANKS * (t + 1) - GROUPS)
                add(1, x_terms[0], True, False)
                pe.wait_ge(s_mom, MOM_BANKS * (t + 1))
                add(1, x_terms[1], False, False)
                pe.wait_ge(s_lin, 2 * (t + 1))
                add(0, z1_terms, True, True).then_inc(s_z1_pe, 1)
                if t == 0:
                    pe.wait_ge(s_bsum, 1)
                    pe.wait_ge(s_fold, FOLDS)
                    turn(LATE, len(turn_banks))
                    turned(pe, len(turn_banks))
                add(1, s_terms + [(bsumT[:, :], mom_l[:, XG - 1, :])], False, True).then_inc(s_z_pe, 1)

            def hidden1(t):
                if t == 0:
                    pe.wait_ge(s_top, 96)
                    pe.wait_ge(s_denseT, 1)
                if t >= 1:
                    pe.wait_ge(s_h1, MID1 * t)
                for k in range(3):
                    if k >= 1:
                        pe.wait_ge(s_z, 2 * t + k)
                    for m in range(MID1):
                        w, x = ((wt1d[:, m * P:(m + 1) * P], denseT[0:DENSE + 1, t * P:(t + 1) * P]) if k == 0
                                else (wt1[:, k - 1, m * P:(m + 1) * P], z_sb[:, k - 1, :]))
                        last = nc.tensor.matmul(h1_ps[:, m * P:(m + 1) * P], w, x, start=(k == 0 and m == 0),
                                                stop=(k == 2), skip_group_check=True)
                        if k == 2:
                            last.then_inc(s_h1_pe, 1)

            def hidden2(t):
                if t >= 1:
                    pe.wait_ge(s_y, t)
                for k in range(MID1):
                    pe.wait_ge(s_h1, MID1 * t + k + 1)
                    for m in range(MID2):
                        last = nc.tensor.matmul(h2_ps[:, m * P:(m + 1) * P], wt2[:, k, m * P:(m + 1) * P],
                                                h1_sb[:, k * P:(k + 1) * P], start=(k == 0 and m == 0),
                                                stop=(k == MID1 - 1), skip_group_check=True)
                last.then_inc(s_h2_pe, 1)

            def outputs(t):
                pe.wait_ge(s_h2, MID2 * (t + 1))
                for m in range(MID2):
                    last = nc.tensor.matmul(y_ps, wt3[:, m:m + 1], h2_sb[:, m, :],
                                            start=(m == 0), stop=(m == MID2 - 1))
                last.then_inc(s_y_pe, 1)

            pe.wait_ge(s_denseT, 1)
            turn(0, FIRST)
            pe.wait_ge(s_other, FIELDS)
            turn(FIRST, EARLY)
            moments(0, {GROUPS: lambda _: turn(EARLY, LATE)})
            contract(0)
            for t in range(1, TILES):
                moments(t, {GROUPS // 2: hidden1, GROUPS: hidden2, 3 * GROUPS // 2: outputs})
                contract(t)
            hidden1(TILES - 1)
            hidden2(TILES - 1)
            outputs(TILES - 1)


_TABLES = [f"tbl_{i}" for i in range(26)]
_INS = ["dense_ctx", "ids", *_TABLES, "W_top1", "b_top1", "W_top2", "b_top2", "W_top3",
        "L0_rec_W1", "L0_rec_b1", "L0_rec_W2", "L0_rec_b2"]


def kernel(**inputs):
    import numpy as _np
    import concourse.bacc as _bacc
    from concourse import mybir as _mybir
    from concourse.bass_utils import run_bass_kernel_spmd as _run

    nc = _bacc.Bacc("TRN2", target_bir_lowering=False, num_devices=1)
    arrays, args = {}, {}
    for name in _INS:
        a = _np.ascontiguousarray(inputs[name])
        arrays[f"in_{name}_dram"] = a
        args[name] = nc.dram_tensor(f"in_{name}_dram", a.shape, _mybir.dt.from_np(a.dtype), kind="ExternalInput").ap()
    batch = inputs["ids"].shape[0]
    out = nc.dram_tensor("out_0_dram", (batch, 1), _mybir.dt.float32, kind="ExternalOutput").ap()
    dlrm_cin_tower(nc, args["dense_ctx"], args["ids"], [args[n] for n in _TABLES], args["W_top1"], args["b_top1"],
                   args["W_top2"], args["b_top2"], args["W_top3"], args["L0_rec_W1"], args["L0_rec_b1"],
                   args["L0_rec_W2"], args["L0_rec_b2"], out)
    r = _run(nc, [arrays], core_ids=[0])
    return r.results[0]["out_0_dram"]
```

```python
from contextlib import ExitStack

import concourse.bass as bass
from concourse import mybir

F32 = mybir.dt.float32
U32 = mybir.dt.uint32
ALU = mybir.AluOpType
ACT = mybir.ActivationFunctionType


def dlrm_cin_tower(nc, dense_ctx, ids, tables, w_top1, b_top1, w_top2, b_top2, w_top3, w1, b1, w2, b2, out):
    P = 128
    BATCH, FIELDS = ids.shape
    K = tables[0].shape[1]
    H1, H2 = w1.shape[0], w2.shape[0]
    DENSE = dense_ctx.shape[1]
    TOP1, TOP2 = w_top2.shape
    TILES = BATCH // P
    QUADS = P // K
    BL = P // QUADS
    C = FIELDS // 2
    ND = C // 2 + 1
    WRAP = ND - 1
    PAIRS = ND * C
    LIN = -(-PAIRS // 32) * 32
    ROWS = LIN + C
    HALF = P // 2
    COLS = FIELDS + 1
    COL = [0, C + 1]
    ONES = [0, C]
    OTHER = [1, 0]
    GROUP = 4
    GROUPS = BL // GROUP
    EXT = 2 * C - 1
    CW = 2 * PAIRS + 1
    XG = -(-C // QUADS)
    MID1 = TOP1 // P
    MID2 = TOP2 // P
    CROSS = C * C
    PER_BANK = 512 // P
    HALVES = 2
    M_HALF = MID1 // HALVES
    LATE_FIELDS = 3
    PARTS = [(0, 0, C), (1, 0, C - LATE_FIELDS), (1, C - LATE_FIELDS, C)]
    assert (P, K, H1, H2) == (128, 32, 128, 128) and FIELDS == 2 * C and C % 2 == 1 and ROWS <= P

    with ExitStack() as ctx:
        def sb(name, shape, dt=F32):
            return ctx.enter_context(nc.sbuf_tensor(name, shape, dt))

        def bank(name):
            return ctx.enter_context(nc.psum_tensor(name, [P, 512], F32))

        def sem(name):
            return ctx.enter_context(nc.semaphore(name))

        ids_sb = sb("ids_sb", [P, TILES, FIELDS], U32)
        rows_sb = sb("rows_sb", [P, TILES, FIELDS * K])
        feat = sb("feat", [P, 2, 2, ROWS + WRAP, BL])
        diag = sb("diag", [P, 2, BL, QUADS, COLS])
        mom_x = sb("mom_x", [ROWS, 2, C + 1, P])
        mom_s = sb("mom_s", [P, C, P])
        mom_l = sb("mom_l", [P, XG, P])
        coef = sb("coef", [P, FIELDS, CW])
        stack = sb("stack", [P, C, 2, HALF])
        coef_x = sb("coef_x", [PAIRS, 2, C, P])
        coef_s = sb("coef_s", [P, C, P])
        startup = feat[:, 1].rearrange("p c r b -> p (c r b)")
        w2_nat = startup[:, 0:H1 * FIELDS].rearrange("h (m l) -> h m l", l=FIELDS)
        w2T = startup[:, H1 * FIELDS:2 * H1 * FIELDS].rearrange("m (l h) -> m l h", l=FIELDS)
        w1_sb = sb("w1_sb", [P, FIELDS, FIELDS])
        w1s = sb("w1s", [P, CW])
        cross = sb("cross", [P, 2, EXT, C])
        cross_l = sb("cross_l", [P, XG * QUADS, 32])
        bsum = sb("bsum", [P, P])
        bsumT = sb("bsumT", [P, P])
        w1T = sb("w1T", [PAIRS, 2, P])
        crossT = sb("crossT", [P, XG, P])
        ident = sb("ident", [P, P])
        bias_in = sb("bias_in", [P, 2])
        bias_z = sb("bias_z", [P, 2])
        dense_sb = sb("dense_sb", [P, TILES, DENSE])
        denseT = sb("denseT", [32, BATCH])
        wt1 = sb("wt1", [P, 2, TOP1])
        wt1d = sb("wt1d", [DENSE + 1, TOP1])
        wt2 = sb("wt2", [P, MID1, TOP2])
        wt3 = sb("wt3", [P, MID2])
        bt2 = sb("bt2", [P, MID2])
        z_sb = sb("z_sb", [P, 2, P])
        h1_sb = sb("h1_sb", [P, MID1 * P])
        h2_sb = sb("h2_sb", [P, MID2, P])
        y_sb = sb("y_sb", [1, BATCH])
        dense1 = sb("dense1", [P, MID1, BATCH])

        ring = [bank(f"ring{i}") for i in range(4)]
        z_ps = [bank(f"z{n + 1}_ps") for n in range(2)]
        h1_ps = bank("h1_ps")
        h2_ps = bank("h2_ps")

        def h1_at(t, m):
            own = t == TILES - 1 and m >= M_HALF
            return (ring[0] if own else h1_ps)[:, m * P:(m + 1) * P]

        def h2_at(t, m):
            return (ring[1] if t == TILES - 1 and m else h2_ps)[:, m * P:(m + 1) * P]

        def y_at(t):
            return ring[2][0:1, 0:P] if t == TILES - 1 else h2_ps[0:1, MID2 * P:(MID2 + 1) * P]

        s_ids = sem("s_ids")
        s_w1 = sem("s_w1")
        s_w2 = sem("s_w2")
        s_dense = sem("s_dense")
        s_top = sem("s_top")
        s_rows = [[sem(f"s_rows{t}_{p}") for p in range(len(PARTS))] for t in range(TILES)]
        s_zero = sem("s_zero")
        s_clear = sem("s_clear")
        s_w1s = sem("s_w1s")
        s_w2T_pe = sem("s_w2T_pe")
        s_w2T = sem("s_w2T")
        s_own_pe = sem("s_own_pe")
        s_own = sem("s_own")
        s_other_pe = sem("s_other_pe")
        s_other = sem("s_other")
        s_bsum = sem("s_bsum")
        s_fold = sem("s_fold")
        s_gap = sem("s_gap")
        s_lin = sem("s_lin")
        s_ct_pe = sem("s_ct_pe")
        s_ct_act = sem("s_ct_act")
        s_ct_dve = sem("s_ct_dve")
        s_dense_pe = sem("s_dense_pe")
        s_denseT = sem("s_denseT")
        s_dense1_pe = sem("s_dense1_pe")
        s_dense1 = sem("s_dense1")
        s_fieldsT = sem("s_fieldsT")
        s_wrap = sem("s_wrap")
        s_pairs = sem("s_pairs")
        s_diag = sem("s_diag")
        s_diag_dve = sem("s_diag_dve")
        s_mom_pe = sem("s_mom_pe")
        s_mom = sem("s_mom")
        s_z1_pe = sem("s_z1_pe")
        s_z_pe = sem("s_z_pe")
        s_z = sem("s_z")
        s_h1_pe = sem("s_h1_pe")
        s_h1_sum = sem("s_h1_sum")
        s_h1 = sem("s_h1")
        s_h2_pe = sem("s_h2_pe")
        s_h2 = sem("s_h2")
        s_y_pe = sem("s_y_pe")
        s_y = sem("s_y")
        s_out = sem("s_out")

        WARM = 22
        BANKS_W2T = -(-FIELDS // PER_BANK)
        OWN_PER_BANK = 2
        OTHER_PER_BANK = 3
        DENSE_AFTER = 5
        own_banks = [range(f, min(f + OWN_PER_BANK, FIELDS)) for f in range(0, FIELDS, OWN_PER_BANK)]
        in_turn = [c * C + a for a in range(C) for c in range(2)]
        other_banks = [in_turn[n:n + OTHER_PER_BANK] for n in range(0, FIELDS, OTHER_PER_BANK)]

        flat = lambda ap: ap.rearrange("r l h -> r (l h)")
        turn_banks = []
        turn_banks.append(([w1s[:, c * PAIRS:(c + 1) * PAIRS] for c in range(2)], PAIRS, flat(w1T[:, :, :])))
        turn_banks.append(([cross_l[:, g * QUADS:(g + 1) * QUADS, :].rearrange("m j i -> m (j i)")
                            for g in range(XG)], P, flat(crossT[:, :, :])))
        for c in range(2):
            for l0 in range(0, C, PER_BANK):
                l1 = min(l0 + PER_BANK, C)
                turn_banks.append(([coef[:, (1 - c) * C + l, c * PAIRS:(c + 1) * PAIRS] for l in range(l0, l1)], PAIRS,
                                   flat(coef_x[:, c, l0:l1, :])))
        for l0 in range(0, C, PER_BANK):
            l1 = min(l0 + PER_BANK, C)
            turn_banks.append(([stack[:, l].rearrange("h c r -> h (c r)") for l in range(l0, l1)], P,
                               flat(coef_s[:, l0:l1, :])))
        turn_banks.append(([bsum[:, :]], P, bsumT[:, :]))

        folds = []
        def other_name(d, s):
            down, up = (s, d - s) if s <= d else (C - s, s - d)
            if s <= d:
                names = [(down, 0, d), (up, s, 0)]
            else:
                names = [(up, d, 0), (down, s, d)]
            return sorted(names, key=lambda n: n[0])
        for d in range(HALF // C, ND):
            for s in range(C):
                for i in range(C):
                    if d * C + i < HALF:
                        continue
                    d2, shift, l_shift = next(n for n in other_name(d, s) if n[0] * C + (i + n[1]) % C < HALF)
                    folds.append((d, s, i, d2, (i + shift) % C, (i + l_shift) % C))
        fold_runs = {}
        for d, s, i, d2, i2, l2 in folds:
            src, dst = ((i + s) % C, d * C + i), (l2, d2 * C + i2)
            runs = fold_runs.setdefault((d2, (l2 - i2) % C), {}).setdefault((d, s), [])
            if runs:
                s0, t0, n = runs[-1]
                if src == (s0[0] + n, s0[1] + n) and dst == (t0[0] + n, t0[1] + n):
                    runs[-1] = (s0, t0, n + 1)
                    continue
            runs.append((src, dst, 1))
        fold_rounds = []
        for by_source in fold_runs.values():
            for n, runs in enumerate(by_source.values()):
                if n == len(fold_rounds):
                    fold_rounds.append([])
                fold_rounds[n] += runs
        FOLDS = 1 + len(fold_rounds)

        MOM_BANKS = 2 * GROUPS

        FIRST = 2
        EARLY = FIRST + 4
        LATE = FIRST + 2 * -(-C // PER_BANK)
        spare = [h1_ps, h2_ps, *z_ps]
        dense_ps = [*z_ps, *ring[2:4]]
        turn_ps = spare[0:FIRST] + 2 * spare + [ring[n % 4] for n in range(len(turn_banks) - LATE)]
        on_act = [n < EARLY or n >= LATE for n in range(len(turn_banks))]

        def turned(eng, upto):
            eng.wait_ge(s_ct_act, sum(on_act[:upto]))
            if upto > sum(on_act[:upto]):
                eng.wait_ge(s_ct_dve, upto - sum(on_act[:upto]))

        def act_quads(t, p):
            return range(QUADS // 2 if t >= 1 and p == len(PARTS) - 1 else QUADS)

        def act_blocks(t):
            return sum(len(act_quads(u, p)) for u in range(t + 1) for p in range(len(PARTS)))

        def diag_block(t, p, q):
            c, f0, f1 = PARTS[p]
            return (diag[q * K:(q + 1) * K, t % 2, :, q, COL[c] + f0:COL[c] + f1].rearrange("p b i -> p i b"),
                    feat[q * K:(q + 1) * K, t % 2, c, LIN + f0:LIN + f1, :])

        block = ctx.enter_context(nc.Block())

        @block.sync
        def _(sp):
            sp.dma_start(ids_sb[:, :, :], ids.bitcast(U32).rearrange("(t p) f -> p t f", p=P)).then_inc(s_ids, 16)
            with nc.allow_non_contiguous_dma(reason="a few hundred biases"):
                sp.dma_start(w2_nat, w2).then_inc(s_w2, 16)
                sp.dma_start(w1_sb[:, :, :], w1).then_inc(s_w1, 16)
                sp.dma_start(bias_in[:, 0:1], b1.rearrange("(p a) -> p a", a=1)).then_inc(s_w1, 16)
                sp.dma_start(bias_in[:, 1:2], b2.rearrange("(p a) -> p a", a=1)).then_inc(s_w1, 16)
                sp.dma_start(dense_sb[:, :, :], dense_ctx.rearrange("(t p) f -> p t f", p=P)).then_inc(s_dense, 16)
                sp.dma_start(wt1d[0:DENSE, :], w_top1[2 * P:2 * P + DENSE, :]).then_inc(s_top, 16)
                sp.dma_start(wt1d[DENSE:DENSE + 1, :], b_top1.rearrange("(a n) -> a n", a=1)).then_inc(s_top, 16)
                sp.dma_start(wt1[:, :, :], w_top1[0:2 * P, :].rearrange("(c p) n -> p c n", p=P)).then_inc(s_top, 16)
                sp.dma_start(wt2[:, :, :], w_top2.rearrange("(c p) n -> p c n", p=P)).then_inc(s_top, 16)
                sp.dma_start(wt3[:, :], w_top3.rearrange("(c p) a -> p (c a)", p=P)).then_inc(s_top, 16)
                sp.dma_start(bt2[:, :], b_top2.rearrange("(c p) -> p c", p=P)).then_inc(s_top, 16)
            sp.wait_ge(s_y, TILES)
            sp.dma_start(out.rearrange("b a -> a b"), y_sb[:, :]).then_inc(s_out, 16)
            sp.wait_ge(s_out, 16)

        @block.gpsimd
        def _(pool):
            nc.gpsimd.memset(ident[:, :], 0.0).then_inc(s_zero, 1)
            pool.wait_ge(s_zero, 1)
            nc.gpsimd.affine_select(out=ident[:, :], in_=ident[:, :], compare_op=ALU.not_equal, fill=1.0, base=0,
                                    pattern=[[-1, P]], channel_multiplier=1).then_inc(s_zero, 1)
            pool.wait_ge(s_ids, 16)
            for t in range(TILES):
                for p, (c, f0, f1) in enumerate(PARTS):
                    for f in range(c * C + f0, c * C + f1):
                        nc.gpsimd.indirect_dma_start(
                            rows_sb[:, t, f * K:(f + 1) * K], None, tables[f],
                            bass.IndirectOffsetOnAxis(ap=ids_sb[:, t, f:f + 1], axis=0)).then_inc(s_rows[t][p], 16)

        @block.scalar
        def _(act):
            def copy_diag(t, p):
                if t <= 1:
                    act.wait_ge(s_clear, 2 * (t + 1))
                if t >= 2:
                    act.wait_ge(s_mom_pe, MOM_BANKS * (t - 1))
                act.wait_ge(s_fieldsT, len(PARTS) * t + p + 1)
                for q in act_quads(t, p):
                    nc.scalar.copy(*diag_block(t, p, q)).then_inc(s_diag, 1)

            def copy_moments(t):
                for n in range(MOM_BANKS):
                    c, g = divmod(n, GROUPS)
                    act.wait_ge(s_mom_pe, MOM_BANKS * t + n + 1)
                    if t == 0 and 1 <= n <= EARLY - FIRST:
                        copy_turned(FIRST + n - 1, FIRST + n)
                    if n == 0 and t >= 1:
                        act.wait_ge(s_z_pe, t)
                        act.wait_ge(s_lin, 2 * t)
                    src = ring[n % 4][:, 0:GROUP * QUADS * COLS].rearrange("r (b q l) -> r b q l", b=GROUP, q=QUADS)
                    samples = lambda ap: ap.rearrange("r l (q g b) -> r g b q l", q=QUADS, b=GROUP)[:, g]
                    x0 = C if c == 0 else 0
                    nc.scalar.copy(samples(mom_x[:, c]), src[0:ROWS, :, :, x0:x0 + C + 1])
                    nc.scalar.copy(samples(mom_s[c * HALF:(c + 1) * HALF]),
                                   src[0:HALF, :, :, COL[c]:COL[c] + C]).then_inc(s_mom, 1)

            def copy_z(t, n):
                if t >= 1 and n == 0:
                    act.wait_ge(s_h1_pe, MID1 * t)
                act.wait_ge(s_z1_pe if n == 0 else s_z_pe, t + 1)
                nc.scalar.activation(z_sb[:, n, :], z_ps[n][:, 0:P], ACT.Identity,
                                     bias=bias_z[:, n:n + 1]).then_inc(s_z, 1)

            def copy_turned(first, end):
                for n in range(first, end):
                    group, rows, dst = turn_banks[n]
                    if on_act[n]:
                        act.wait_ge(s_ct_pe, n + 1)
                        nc.scalar.copy(dst, turn_ps[n][0:rows, 0:len(group) * P]).then_inc(s_ct_act, 1)

            def copy_dense(first, end):
                for m in range(first, end):
                    act.wait_ge(s_dense1_pe, m + 1)
                    nc.scalar.copy(dense1[:, m, :], dense_ps[m][:, 0:BATCH]).then_inc(s_dense1, 1)

            for n in range(BANKS_W2T):
                f0, f1 = n * PER_BANK, min((n + 1) * PER_BANK, FIELDS)
                act.wait_ge(s_w2T_pe, n + 1)
                nc.scalar.copy(w2T[:, f0:f1, :].rearrange("m l h -> m (l h)"),
                               ring[n % 4][:, 0:(f1 - f0) * P]).then_inc(s_w2T, 1)
            for n, fs in enumerate(own_banks):
                act.wait_ge(s_own_pe, n + 1)
                nc.scalar.copy(coef[:, fs[0]:fs[-1] + 1, :].rearrange("h l r -> h (l r)"),
                               ring[n % 4][:, 0:len(fs) * CW]).then_inc(s_own, 1)
            copy_diag(0, 0)
            copy_dense(0, MID1 // 2)
            copy_turned(0, FIRST)
            for p in range(1, len(PARTS)):
                copy_diag(0, p)
            copy_dense(MID1 // 2, MID1)
            copy_moments(0)
            copy_turned(LATE, len(turn_banks))
            for t in range(1, TILES):
                copy_diag(t, 0)
                if t == 1:
                    act.wait_ge(s_w1s, 1)
                copy_z(t - 1, 0)
                copy_diag(t, 1)
                if t < TILES - 1:
                    copy_diag(t, 2)
                copy_z(t - 1, 1)
                if t == TILES - 1:
                    copy_diag(t, 2)
                copy_moments(t)
            for n in range(2):
                copy_z(TILES - 1, n)

        @block.vector
        def _(dve):
            def clear_diag(u):
                nc.vector.memset(diag[:, u].rearrange("p b q l -> p (b q l)"), 0.0).then_inc(s_clear, 1)
                dve.wait_ge(s_clear, 2 * u + 1)
                for q in range(QUADS):
                    last = nc.vector.memset(diag[q * K:(q + 1) * K, u, :, q, C], 1.0)
                last.then_inc(s_clear, 1)

            clear_diag(0)
            dve.wait_ge(s_w1, 48)
            nc.vector.tensor_scalar(bias_z[:, :], bias_in[:, :], float(K), None, ALU.mult).then_inc(s_w1s, 1)
            whole = w1_sb[:, :, :].rearrange("m i j -> m (i j)")
            clique_step = C * (FIELDS + 1)

            def diagonal(i0, j0, n):
                at = whole[:, i0 * FIELDS + j0:].unsqueeze(1)
                return bass.AP(at.tensor, at.offset, [list(at.ap[0]), [clique_step, 2], [FIELDS + 1, n]])

            for d in range(ND):
                for i0, i1 in ((0, C - d), (C - d, C)):
                    if i0 == i1:
                        continue
                    j0 = (i0 + d) % C
                    dst = w1s[:, 0:2 * PAIRS].rearrange("m (c r) -> m c r", c=2)[:, :, d * C + i0:d * C + i1]
                    if d == 0:
                        nc.vector.tensor_copy(dst, diagonal(i0, j0, i1 - i0))
                    else:
                        nc.vector.tensor_tensor(dst, diagonal(i0, j0, i1 - i0), diagonal(j0, i0, i1 - i0), ALU.add)
            nc.vector.tensor_copy(w1s[:, 2 * PAIRS:CW], bias_in[:, 0:1]).then_inc(s_w1s, 1)
            for c in range(2):
                x = slice(c * C, (c + 1) * C)
                y = slice((1 - c) * C, (2 - c) * C)
                nc.vector.tensor_tensor(cross[:, c, WRAP:WRAP + C, :], w1_sb[:, x, y],
                                        w1_sb[:, y, x].rearrange("m j i -> m i j"), ALU.add).then_inc(s_w1s, 1)
            dve.wait_ge(s_w1s, 4)
            for c in range(2):
                nc.vector.tensor_copy(cross[:, c, 0:WRAP, :], cross[:, c, C:C + WRAP, :])
                nc.vector.tensor_copy(cross[:, c, WRAP + C:EXT, :], cross[:, c, WRAP:2 * WRAP, :]).then_inc(s_w1s, 1)
            nc.vector.memset(cross_l[:, :, :], 0.0)
            nc.vector.memset(bsum[:, :], 0.0)
            nc.vector.memset(mom_l[:, :, :], 0.0)
            nc.vector.memset(denseT[:, :], 1.0).then_inc(s_w1s, 1)
            nc.vector.memset(feat[:, 0, :, PAIRS:LIN, :], 0.0).then_inc(s_gap, 1)
            dve.wait_ge(s_w1s, 7)
            nc.vector.tensor_copy(cross_l[:, 0:C, 0:C], cross[:, 0, WRAP:WRAP + C, :].rearrange("m i l -> m l i"))
            clear_diag(1)
            dve.wait_ge(s_dense_pe, 1)
            nc.vector.tensor_copy(denseT[0:DENSE, :], h1_ps[0:DENSE, 0:BATCH]).then_inc(s_denseT, 1)

            def pair_rows(t, c):
                return feat[:, t % 2, c].rearrange("p r b -> p (r b)")

            def fields_of(t, p):
                if t == 1 and p == 0:
                    dve.wait_ge(s_other_pe, len(other_banks))
                    nc.vector.memset(feat[:, 1, :, PAIRS:LIN, :], 0.0).then_inc(s_gap, 1)
                if t >= 2 and p == 0:
                    dve.wait_ge(s_mom_pe, MOM_BANKS * (t - 1))
                    dve.wait_ge(s_diag, act_blocks(t - 2))
                c, f0, f1 = PARTS[p]
                f = pair_rows(t, c)
                dve.wait_ge(s_rows[t][p], 16 * (f1 - f0))
                nc.vector.transpose(f[:, (LIN + f0) * BL:(LIN + f1) * BL],
                                    rows_sb[:, t, (c * C + f0) * K:(c * C + f1) * K]).then_inc(s_fieldsT, 1)
                if len(act_quads(t, p)) < QUADS:
                    dve.wait_ge(s_fieldsT, len(PARTS) * t + p + 1)
                    for q in range(QUADS):
                        if q not in act_quads(t, p):
                            last = nc.vector.tensor_copy(*diag_block(t, p, q))
                    last.then_inc(s_diag_dve, 1)

            def repeat_of(t, c):
                f = pair_rows(t, c)
                dve.wait_ge(s_fieldsT, len(PARTS) * t + (1, len(PARTS))[c])
                nc.vector.tensor_copy(f[:, ROWS * BL:(ROWS + WRAP) * BL],
                                      f[:, LIN * BL:(LIN + WRAP) * BL]).then_inc(s_wrap, 1)
                dve.wait_ge(s_wrap, 2 * t + c + 1)

            def products_of(t, c, half):
                n = BL // HALVES
                one = feat[:, t % 2, c, LIN:ROWS, half * n:(half + 1) * n]
                two = bass.AP(one.tensor, one.offset, [list(one.ap[0]), [BL, ND], [BL, C], [1, n]])
                dst = feat[:, t % 2, c, 0:PAIRS, half * n:(half + 1) * n].rearrange("p (d i) b -> p d i b", d=ND)
                nc.vector.tensor_tensor(dst, one.unsqueeze(1).to_broadcast([P, ND, C, n]), two,
                                        ALU.mult).then_inc(s_pairs, 1)

            def copy_lin(t):
                for c in range(2):
                    dve.wait_ge(s_mom, MOM_BANKS * (t + 1) - GROUPS * (1 - c))
                    if t >= 1 and c == 0:
                        dve.wait_ge(s_z_pe, t)
                    if c == 0:
                        for j in range(QUADS):
                            n = len(range(j, C, QUADS))
                            nc.vector.tensor_copy(mom_l[32 * j:32 * j + C, 0:n, :],
                                                  mom_x[LIN:ROWS, 0, OTHER[0] + j:C + 1:QUADS, :])
                    q = 32 * (1 + c)
                    nc.vector.tensor_copy(mom_l[q:q + C, XG - 1, :], mom_x[LIN:ROWS, c, ONES[c], :]).then_inc(s_lin, 1)

            def relu1(t):
                half = lambda g: slice(g * M_HALF * P, (g + 1) * M_HALF * P)
                if t == 0:
                    dve.wait_ge(s_dense1, MID1)
                for g in range(HALVES):
                    dve.wait_ge(s_h1_pe, MID1 * t + (M_HALF * (g + 1) if t == TILES - 1 else MID1))
                    if t >= 1 and g == 0:
                        dve.wait_ge(s_h2_pe, MID2 * t)
                    src = (ring[0] if t == TILES - 1 and g else h1_ps)[:, half(g)]
                    by_part = lambda ap: ap.rearrange("p (m b) -> p m b", m=M_HALF)
                    nc.vector.tensor_tensor(
                        by_part(h1_sb[:, half(g)]), by_part(src),
                        dense1[:, g * M_HALF:(g + 1) * M_HALF, t * P:(t + 1) * P], ALU.add).then_inc(s_h1_sum, 1)
                    dve.wait_ge(s_h1_sum, HALVES * t + g + 1)
                    nc.vector.tensor_scalar(h1_sb[:, half(g)], h1_sb[:, half(g)], 0.0, None,
                                            ALU.max).then_inc(s_h1, 1)

            def relu2(t):
                if t >= 1:
                    dve.wait_ge(s_y_pe, t)
                for m in range(MID2):
                    dve.wait_ge(s_h2_pe, MID2 * t + (m + 1 if t == TILES - 1 else MID2))
                    nc.vector.tensor_scalar(h2_sb[:, m, :], h2_at(t, m), bt2[:, m:m + 1], 0.0,
                                            ALU.add, ALU.max).then_inc(s_h2, 1)

            fields_of(0, 0)
            repeat_of(0, 0)
            for half in range(HALVES):
                products_of(0, 0, half)
            done = 0
            for n, fs in enumerate(other_banks):
                dve.wait_ge(s_other_pe, n + 1)
                if n == 0:
                    dve.wait_ge(s_own, len(own_banks))
                for k, f in enumerate(fs):
                    c, a = divmod(f, C)
                    got = ring[(len(own_banks) + n) % 4][:, k * CROSS:(k + 1) * CROSS]
                    got = got.rearrange("h (u l) -> h u l", u=C)
                    ls = slice((1 - c) * C, (2 - c) * C)
                    table = coef[:, ls, c * PAIRS:(c + 1) * PAIRS].rearrange("h l r -> h r l")
                    if done >= 2:
                        dve.wait_ge(s_other, done - 1)
                    parts = [(table[:, a:a + C * (ND - 1) + 1:C, :], got[:, WRAP:, :])]
                    down = min(WRAP, a)
                    if down:
                        r0 = (C - 1) * 1 + a
                        parts.append((table[:, r0:r0 + (C - 1) * (down - 1) + 1:C - 1, :],
                                      got[:, WRAP - 1 - (down - 1):WRAP, :][:, ::-1, :]))
                    if down < WRAP:
                        r0 = (C - 1) * (down + 1) + C + a
                        cnt = WRAP - down
                        parts.append((table[:, r0:r0 + (C - 1) * (cnt - 1) + 1:C - 1, :],
                                      got[:, 0:cnt, :][:, ::-1, :]))
                    for dst, src in parts:
                        last = nc.vector.tensor_tensor(dst, dst, src, ALU.add)
                    last.then_inc(s_other, 1)
                    done += 1

            def copy_turned(first, end):
                for n in range(first, end):
                    group, rows, dst = turn_banks[n]
                    if not on_act[n]:
                        dve.wait_ge(s_ct_pe, n + 1)
                        nc.vector.tensor_copy(dst, turn_ps[n][0:rows, 0:len(group) * P]).then_inc(s_ct_dve, 1)

            for p in range(1, len(PARTS)):
                fields_of(0, p)
            repeat_of(0, 1)
            for half in range(HALVES):
                products_of(0, 1, half)
            copy_turned(EARLY, LATE)
            for c in range(2):
                q = 32 * (1 + c)
                last = nc.vector.tensor_copy(bsum[:, q:q + C], coef[:, c * C:(c + 1) * C, 2 * PAIRS])
            last.then_inc(s_bsum, 1)

            def steps(ap, clique_step, step, n):
                return bass.AP(ap.tensor, ap.offset, [list(ap.ap[0]), [clique_step, 2], [step, n]])

            def fold():
                rows = lambda c: coef[:, c * C:(c + 1) * C, c * PAIRS:c * PAIRS + HALF]
                for c in range(2):
                    last = nc.vector.tensor_copy(stack[:, :, c, :], rows(c))
                last.then_inc(s_fold, 1)
                dve.wait_ge(s_fold, 1)
                for n, runs in enumerate(fold_rounds):
                    if n >= 1:
                        dve.wait_ge(s_fold, n + 1)
                    for (l1, r1), (l2, r2), count in runs:
                        dst = steps(stack[:, l2, 0, r2:], HALF, 2 * HALF + 1, count)
                        src = steps(coef[:, l1, r1:], C * CW + PAIRS, CW + 1, count)
                        last = nc.vector.tensor_tensor(dst, dst, src, ALU.add)
                    last.then_inc(s_fold, 1)

            fold()
            copy_lin(0)

            def finish(t):
                relu1(t)
                relu2(t)
                dve.wait_ge(s_y_pe, t + 1)
                nc.vector.tensor_copy(y_sb[:, t * P:(t + 1) * P], y_at(t)).then_inc(s_y, 1)

            for t in range(1, TILES):
                fields_of(t, 0)
                repeat_of(t, 0)
                for half in range(HALVES):
                    products_of(t, 0, half)
                if t >= 2:
                    copy_lin(t - 1)
                for p in range(1, len(PARTS)):
                    fields_of(t, p)
                repeat_of(t, 1)
                for half in range(HALVES):
                    products_of(t, 1, half)
                if t == 1:
                    dve.wait_ge(s_top, 96)
                finish(t - 1)
            copy_lin(TILES - 1)
            finish(TILES - 1)

        @block.tensor
        def _(pe):
            pe.wait_ge(s_zero, 2)
            for n in range(WARM):
                nc.tensor.matmul(z_ps[0][:, 0:P], ident[:, :], ident[:, :], start=True, stop=True)
            pe.wait_ge(s_w2, 16)
            for n in range(BANKS_W2T):
                if n >= 4:
                    pe.wait_ge(s_w2T, n - 3)
                for k, f in enumerate(range(n * PER_BANK, min((n + 1) * PER_BANK, FIELDS))):
                    last = nc.tensor.transpose(ring[n % 4][:, k * P:(k + 1) * P], w2_nat[:, :, f], ident[:, :])
                last.then_inc(s_w2T_pe, 1)
            pe.wait_ge(s_dense, 16)
            for t in range(TILES):
                last = nc.tensor.transpose(h1_ps[0:DENSE, t * P:(t + 1) * P], dense_sb[:, t, :], ident[:, :])
            last.then_inc(s_dense_pe, 1)

            def dense_part(m):
                if m == 0:
                    pe.wait_ge(s_top, 96)
                    pe.wait_ge(s_denseT, 1)
                nc.tensor.matmul(dense_ps[m][:, 0:BATCH], wt1d[0:DENSE + 1, m * P:(m + 1) * P],
                                 denseT[0:DENSE + 1, :], start=True, stop=True).then_inc(s_dense1_pe, 1)

            pe.wait_ge(s_w1s, 2)
            for n, fs in enumerate(own_banks):
                pe.wait_ge(s_w2T, min(BANKS_W2T, BANKS_W2T - 2 + n))
                if n >= 4:
                    pe.wait_ge(s_own, n - 3)
                for k, f in enumerate(fs):
                    last = nc.tensor.matmul(ring[n % 4][:, k * CW:(k + 1) * CW], w2T[:, f, :], w1s[:, :],
                                            start=True, stop=True)
                last.then_inc(s_own_pe, 1)
            pe.wait_ge(s_w1s, 6)
            for n, fs in enumerate(other_banks):
                if n < 4:
                    pe.wait_ge(s_own, len(own_banks) - 3 + n)
                else:
                    pe.wait_ge(s_other, OTHER_PER_BANK * (n - 3))
                for k, f in enumerate(fs):
                    c, a = divmod(f, C)
                    last = nc.tensor.matmul(ring[(len(own_banks) + n) % 4][:, k * CROSS:(k + 1) * CROSS],
                                            w2T[:, f, :], cross[:, c, a:a + C, :].rearrange("m x l -> m (x l)"),
                                            start=True, stop=True)
                last.then_inc(s_other_pe, 1)
                if n == DENSE_AFTER:
                    dense_part(0)

            def turn(first, end):
                for n in range(first, end):
                    before = [k for k in range(n) if turn_ps[k] is turn_ps[n]]
                    if before:
                        turned(pe, before[-1] + 1)
                    for k, src in enumerate(turn_banks[n][0]):
                        last = nc.tensor.transpose(turn_ps[n][0:turn_banks[n][1], k * P:(k + 1) * P], src, ident[:, :])
                    last.then_inc(s_ct_pe, 1)

            def moments(t):
                if t <= 1:
                    pe.wait_ge(s_gap, t + 1)
                for n in range(MOM_BANKS):
                    c, g = divmod(n, GROUPS)
                    if t == 0 and n == GROUPS:
                        turn(EARLY, LATE)
                    if t >= 1:
                        mlp_between(t - 1, n)
                    if n == 0:
                        pe.wait_ge(s_diag, act_blocks(t))
                        if t >= 1:
                            pe.wait_ge(s_diag_dve, t)
                    half, at = divmod(g, GROUPS // HALVES)
                    if at == 0:
                        pe.wait_ge(s_pairs, HALVES * (2 * t + c) + half + 1)
                    if t == 0 and n == 2:
                        pe.wait_ge(s_dense1, MID1)
                    if t >= 1 or n >= 4:
                        pe.wait_ge(s_mom, MOM_BANKS * t + n - 3)
                    for b in range(GROUP):
                        s = g * GROUP + b
                        last = nc.tensor.matmul(ring[n % 4][0:ROWS, b * QUADS * COLS:(b + 1) * QUADS * COLS],
                                                feat[:, t % 2, c, 0:ROWS, s],
                                                diag[:, t % 2, s].rearrange("p q l -> p (q l)"),
                                                start=True, stop=True)
                    last.then_inc(s_mom_pe, 1)

            def contract(t):
                if t >= 1:
                    pe.wait_ge(s_z, 2 * t)
                x_terms = [[(coef_x[:, c, l, :], mom_x[0:PAIRS, c, OTHER[c] + l, :]) for l in range(C)]
                           for c in range(2)]
                s_terms = [(coef_s[:, l, :], mom_s[:, l, :]) for l in range(C)]
                z1_terms = [(w1T[:, c, :], mom_x[0:PAIRS, c, ONES[c], :]) for c in range(2)]
                z1_terms += [(crossT[:, g, :], mom_l[:, g, :]) for g in range(XG)]

                def add(n, terms, start, stop):
                    for k, (w, m) in enumerate(terms):
                        last = nc.tensor.matmul(z_ps[n][:, 0:P], w, m, start=(start and k == 0),
                                                stop=(stop and k == len(terms) - 1))
                    return last

                if t == 0:
                    turned(pe, LATE)
                pe.wait_ge(s_mom, MOM_BANKS * (t + 1) - GROUPS)
                add(1, x_terms[0], True, False)
                pe.wait_ge(s_mom, MOM_BANKS * (t + 1))
                add(1, x_terms[1], False, False)
                if t == 0:
                    pe.wait_ge(s_bsum, 1)
                    pe.wait_ge(s_fold, FOLDS)
                    turn(LATE, len(turn_banks))
                pe.wait_ge(s_lin, 2 * (t + 1))
                add(0, z1_terms, True, True).then_inc(s_z1_pe, 1)
                if t == 0:
                    turned(pe, len(turn_banks))
                add(1, s_terms + [(bsumT[:, :], mom_l[:, XG - 1, :])], False, True).then_inc(s_z_pe, 1)

            def hidden1(t, k):
                if t >= 1 and k == 0:
                    pe.wait_ge(s_h1, HALVES * t)
                firsts = (0, M_HALF) if t == TILES - 1 else (0,)
                pe.wait_ge(s_z, 2 * t + k + 1)
                for m in range(MID1):
                    last = nc.tensor.matmul(h1_at(t, m), wt1[:, k, m * P:(m + 1) * P], z_sb[:, k, :],
                                            start=(k == 0 and m in firsts), stop=(k == 1), skip_group_check=True)
                    if k == 1:
                        last.then_inc(s_h1_pe, 1)

            def hidden2(t):
                if t >= 1:
                    pe.wait_ge(s_y, t)
                apart = t == TILES - 1
                for half in range(HALVES):
                    pe.wait_ge(s_h1, HALVES * t + half + 1)
                    for m in range(MID2):
                        for k in range(half * M_HALF, (half + 1) * M_HALF):
                            last = nc.tensor.matmul(h2_at(t, m), wt2[:, k, m * P:(m + 1) * P],
                                                    h1_sb[:, k * P:(k + 1) * P], start=(k == 0 and (m == 0 or apart)),
                                                    stop=(k == MID1 - 1), skip_group_check=True)
                        if half == HALVES - 1:
                            last.then_inc(s_h2_pe, 1)

            def outputs(t):
                for m in range(MID2):
                    pe.wait_ge(s_h2, MID2 * t + (m + 1 if t == TILES - 1 else MID2))
                    last = nc.tensor.matmul(y_at(t), wt3[:, m:m + 1], h2_sb[:, m, :],
                                            start=(m == 0), stop=(m == MID2 - 1))
                last.then_inc(s_y_pe, 1)

            def mlp_between(t, n):
                last = t == TILES - 2
                if n == 0:
                    hidden1(t, 0)
                if n == (0 if last else GROUPS // 2):
                    hidden1(t, 1)
                if n == (GROUPS - 2 if last else GROUPS):
                    hidden2(t)
                if n == 3 * GROUPS // 2:
                    outputs(t)

            dense_part(1)
            turn(0, FIRST)
            pe.wait_ge(s_other, FIELDS)
            pe.wait_ge(s_dense1, 2)
            turn(FIRST, EARLY)
            for m in range(2, MID1):
                dense_part(m)
            moments(0)
            contract(0)
            for t in range(1, TILES):
                moments(t)
                contract(t)
            for k in range(2):
                hidden1(TILES - 1, k)
            hidden2(TILES - 1)
            outputs(TILES - 1)


_TABLES = [f"tbl_{i}" for i in range(26)]
_INS = ["dense_ctx", "ids", *_TABLES, "W_top1", "b_top1", "W_top2", "b_top2", "W_top3",
        "L0_rec_W1", "L0_rec_b1", "L0_rec_W2", "L0_rec_b2"]


def kernel(**inputs):
    import numpy as _np
    import concourse.bacc as _bacc
    from concourse import mybir as _mybir
    from concourse.bass_utils import run_bass_kernel_spmd as _run

    nc = _bacc.Bacc("TRN2", target_bir_lowering=False, num_devices=1)
    arrays, args = {}, {}
    for name in _INS:
        a = _np.ascontiguousarray(inputs[name])
        arrays[f"in_{name}_dram"] = a
        args[name] = nc.dram_tensor(f"in_{name}_dram", a.shape, _mybir.dt.from_np(a.dtype), kind="ExternalInput").ap()
    batch = inputs["ids"].shape[0]
    out = nc.dram_tensor("out_0_dram", (batch, 1), _mybir.dt.float32, kind="ExternalOutput").ap()
    dlrm_cin_tower(nc, args["dense_ctx"], args["ids"], [args[n] for n in _TABLES], args["W_top1"], args["b_top1"],
                   args["W_top2"], args["b_top2"], args["W_top3"], args["L0_rec_W1"], args["L0_rec_b1"],
                   args["L0_rec_W2"], args["L0_rec_b2"], out)
    r = _run(nc, [arrays], core_ids=[0])
    return r.results[0]["out_0_dram"]
```
